# Optimizing a Trainium2 kernel written in Bass

```python
import numpy as np
import jax
import jax.numpy as jnp

def _softmax(x, axis=-1):
    return jax.nn.softmax(x, axis=axis)

def _gelu(x):
    return jax.nn.gelu(x, approximate=True)

def _silu(x):
    return jax.nn.silu(x)

def _sigmoid(x):
    return jax.nn.sigmoid(x)

def _layernorm(x, axis=-1, eps=1e-05):
    m = jnp.mean(x, axis=axis, keepdims=True)
    v = jnp.var(x, axis=axis, keepdims=True)
    return (x - m) / jnp.sqrt(v + eps)

def _scatter_add(tgt, idx, src, axis=0):
    return tgt.at[idx].add(src)

def _segment_sum(src, seg, n):
    return jax.ops.segment_sum(src, seg, n)
kernel_name = 'mk_vit_tower_d1_tok_img768_r4_28b017'

def setup_inputs(seed: int=0):
    np.random.seed(seed)
    _w = jnp.asarray

    def _rec_inputs():
        import jax
        import jax.numpy as jnp
        _rk = jax.random.key(seed)
        x = -0.000356955 + 1 * jax.random.normal(jax.random.fold_in(_rk, 1), (64, 3, 224, 224), jnp.float32)
        return x
    x = _rec_inputs()

    def _L0_tok_setup():
        import jax, jax.numpy as jnp
        import numpy as np
        C, H, W_IMG = (3, 224, 224)
        NP = 14
        PS = H // NP
        D_IN = C * PS * PS
        D = 192
        SEQ = NP * NP + 1
        B = 128

        def _sinusoidal_pos_embed(seq_len, d):
            i = np.arange(seq_len, dtype=np.float64)[:, None]
            j = np.arange(d, dtype=np.float64)[None, :]
            angle = i / np.power(10000.0, (j - j % 2) / d)
            pe = np.where(j % 2 == 0, np.sin(angle), np.cos(angle))
            return jnp.asarray(pe, dtype=jnp.float32)
        key = jax.random.key(seed)
        kx, kw, kc = jax.random.split(key, 3)
        x = jax.random.normal(kx, (B, C, H, W_IMG), dtype=jnp.float32)
        W = jax.random.normal(kw, (D, D_IN), dtype=jnp.float32) * 0.02
        b = jnp.zeros((D,), dtype=jnp.float32)
        class_token = jax.random.uniform(kc, (1, D), dtype=jnp.float32)
        pos_embed = _sinusoidal_pos_embed(SEQ, D)
        return {'x': x, 'W': W, 'b': b, 'class_token': class_token, 'pos_embed': pos_embed}
    _L0_tok_all = _L0_tok_setup()
    _L0_tok_in = {k: v for k, v in _L0_tok_all.items() if k in ('W', 'b', 'class_token', 'pos_embed')}
    del _L0_tok_all

    def _L0_attn_setup():
        import jax, jax.numpy as jnp
        import numpy as np
        MAX_DIST = 100

        def _pos_bias(rel_emb, length):
            emb_sum = rel_emb[..., 0].sum(axis=-1)
            pos = jnp.arange(length)
            rel = pos[None, :] - pos[:, None]
            idx = jnp.clip(rel, -(MAX_DIST - 1), MAX_DIST - 1) + MAX_DIST - 1
            return emb_sum[:, idx]
        key = jax.random.key(seed)
        ks = jax.random.split(key, 6)
        b, s, e, h, d = (4, 512, 192, 8, 96)
        return {'x': jax.random.normal(ks[0], (b, s, e), dtype=jnp.float32), 'w_q': jax.random.normal(ks[1], (h, e, d), dtype=jnp.float32) * 0.02, 'w_k': jax.random.normal(ks[2], (h, e, d), dtype=jnp.float32) * 0.02, 'w_v': jax.random.normal(ks[3], (h, e, d), dtype=jnp.float32) * 0.02, 'w_o': jax.random.normal(ks[4], (h, d, e), dtype=jnp.float32) * 0.02, 'rel_emb': jax.random.normal(ks[5], (h, 2 * MAX_DIST - 1, d, 1), dtype=jnp.float32) * 0.02}
    _L0_attn_all = _L0_attn_setup()
    _L0_attn_in = {k: v for k, v in _L0_attn_all.items() if k in ('w_q', 'w_k', 'w_v', 'w_o', 'rel_emb')}
    del _L0_attn_all

    def _L0_ffn_setup():
        import jax, jax.numpy as jnp
        import numpy as np
        DIM = 192
        H = 12
        HD = 64
        SHARED = 2
        ROUTED = 2
        E_ROUTED = H - SHARED
        LN_EPS = 1e-05

        def _layernorm(x, w, b):
            m = x.mean(-1, keepdims=True)
            v = ((x - m) ** 2).mean(-1, keepdims=True)
            return (x - m) * jax.lax.rsqrt(v + LN_EPS) * w + b
        key = jax.random.key(seed)
        ks = jax.random.split(key, 12)
        B, N = (4, 512)
        s = 0.02
        return {'x': jax.random.normal(ks[0], (B, N, DIM), jnp.float32), 'qkv_w': jax.random.normal(ks[1], (DIM, 3 * H * HD), jnp.float32) * s, 'qkv_b': jnp.zeros((3 * H * HD,), jnp.float32), 'q_norm_w': jnp.ones((HD,), jnp.float32), 'q_norm_b': jnp.zeros((HD,), jnp.float32), 'k_norm_w': jnp.ones((HD,), jnp.float32), 'k_norm_b': jnp.zeros((HD,), jnp.float32), 'wg_w': jax.random.normal(ks[2], (DIM, E_ROUTED), jnp.float32) * s, 'wg0_w': jax.random.normal(ks[3], (DIM, 2), jnp.float32) * s, 'wg1_w': jax.random.normal(ks[4], (DIM, SHARED), jnp.float32) * s, 'proj_w': jax.random.normal(ks[5], (H * HD, DIM), jnp.float32) * s, 'proj_b': jnp.zeros((DIM,), jnp.float32)}
    _L0_ffn_all = _L0_ffn_setup()
    _L0_ffn_in = {k: v for k, v in _L0_ffn_all.items() if k in ('qkv_w', 'qkv_b', 'q_norm_w', 'q_norm_b', 'k_norm_w', 'k_norm_b', 'wg_w', 'wg0_w', 'wg1_w', 'proj_w', 'proj_b')}
    del _L0_ffn_all
    return {'x': x, 'L0_tok_W': _L0_tok_in['W'], 'L0_tok_b': _L0_tok_in['b'], 'L0_tok_class_token': _L0_tok_in['class_token'], 'L0_tok_pos_embed': _L0_tok_in['pos_embed'], 'L0_attn_w_q': _L0_attn_in['w_q'], 'L0_attn_w_k': _L0_attn_in['w_k'], 'L0_attn_w_v': _L0_attn_in['w_v'], 'L0_attn_w_o': _L0_attn_in['w_o'], 'L0_attn_rel_emb': _L0_attn_in['rel_emb'], 'L0_ffn_qkv_w': _L0_ffn_in['qkv_w'], 'L0_ffn_qkv_b': _L0_ffn_in['qkv_b'], 'L0_ffn_q_norm_w': _L0_ffn_in['q_norm_w'], 'L0_ffn_q_norm_b': _L0_ffn_in['q_norm_b'], 'L0_ffn_k_norm_w': _L0_ffn_in['k_norm_w'], 'L0_ffn_k_norm_b': _L0_ffn_in['k_norm_b'], 'L0_ffn_wg_w': _L0_ffn_in['wg_w'], 'L0_ffn_wg0_w': _L0_ffn_in['wg0_w'], 'L0_ffn_wg1_w': _L0_ffn_in['wg1_w'], 'L0_ffn_proj_w': _L0_ffn_in['proj_w'], 'L0_ffn_proj_b': _L0_ffn_in['proj_b']}

def reference(x, L0_tok_W, L0_tok_b, L0_tok_class_token, L0_tok_pos_embed, L0_attn_w_q, L0_attn_w_k, L0_attn_w_v, L0_attn_w_o, L0_attn_rel_emb, L0_ffn_qkv_w, L0_ffn_qkv_b, L0_ffn_q_norm_w, L0_ffn_q_norm_b, L0_ffn_k_norm_w, L0_ffn_k_norm_b, L0_ffn_wg_w, L0_ffn_wg0_w, L0_ffn_wg1_w, L0_ffn_proj_w, L0_ffn_proj_b):
    import jax
    import jax.numpy as jnp

    def _L0_tok_ref(x, W, b, class_token, pos_embed):
        import jax, jax.numpy as jnp
        import numpy as np
        C, H, W_IMG = (3, 224, 224)
        NP = 14
        PS = H // NP
        D_IN = C * PS * PS
        D = 192
        SEQ = NP * NP + 1
        B = 128

        def _sinusoidal_pos_embed(seq_len, d):
            i = np.arange(seq_len, dtype=np.float64)[:, None]
            j = np.arange(d, dtype=np.float64)[None, :]
            angle = i / np.power(10000.0, (j - j % 2) / d)
            pe = np.where(j % 2 == 0, np.sin(angle), np.cos(angle))
            return jnp.asarray(pe, dtype=jnp.float32)
        n = x.shape[0]
        p = x.reshape(n, C, NP, PS, NP, PS)
        p = p.transpose(0, 2, 4, 1, 3, 5).reshape(n, NP * NP, D_IN)
        tokens = jnp.einsum('npd,hd->nph', p, W) + b
        cls = jnp.broadcast_to(class_token[None], (n, 1, D))
        tokens = jnp.concatenate([cls, tokens], axis=1)
        return tokens + pos_embed[None]

    def _L0_attn_ref(x, w_q, w_k, w_v, w_o, rel_emb):
        import jax, jax.numpy as jnp
        import numpy as np
        MAX_DIST = 100

        def _pos_bias(rel_emb, length):
            emb_sum = rel_emb[..., 0].sum(axis=-1)
            pos = jnp.arange(length)
            rel = pos[None, :] - pos[:, None]
            idx = jnp.clip(rel, -(MAX_DIST - 1), MAX_DIST - 1) + MAX_DIST - 1
            return emb_sum[:, idx]
        b, s, e = x.shape
        d = w_q.shape[-1]
        q = jnp.einsum('bse,hed->bhsd', x, w_q)
        k = jnp.einsum('bse,hed->bhsd', x, w_k)
        v = jnp.einsum('bse,hed->bhsd', x, w_v)
        scale = d ** (-0.5)
        logits = jnp.einsum('bhqd,bhkd->bhqk', q, k) * scale
        logits = logits + _pos_bias(rel_emb, s)[None]
        attn = jax.nn.softmax(logits, axis=-1)
        ctx = jnp.einsum('bhqk,bhkd->bhqd', attn, v)
        return jnp.einsum('bhsd,hde->bse', ctx, w_o)

    def _L0_ffn_ref(x, qkv_w, qkv_b, q_norm_w, q_norm_b, k_norm_w, k_norm_b, wg_w, wg0_w, wg1_w, proj_w, proj_b):
        import jax, jax.numpy as jnp
        import numpy as np
        DIM = 192
        H = 12
        HD = 64
        SHARED = 2
        ROUTED = 2
        E_ROUTED = H - SHARED
        LN_EPS = 1e-05

        def _layernorm(x, w, b):
            m = x.mean(-1, keepdims=True)
            v = ((x - m) ** 2).mean(-1, keepdims=True)
            return (x - m) * jax.lax.rsqrt(v + LN_EPS) * w + b
        B, N, C = x.shape
        scale = HD ** (-0.5)
        gates = jax.nn.softmax(x @ wg_w, axis=-1)
        _, idx = jax.lax.top_k(gates, ROUTED)
        mask = jax.nn.one_hot(idx, E_ROUTED, dtype=gates.dtype).sum(-2)
        rg = gates * mask
        denom = jnp.clip(rg.sum(-1, keepdims=True), jnp.finfo(rg.dtype).eps, None)
        routed_gates = rg / denom * ROUTED
        qkv = (x @ qkv_w + qkv_b).reshape(B, N, 3, H, HD)
        qkv = jnp.transpose(qkv, (2, 0, 3, 1, 4))
        q, k, v = (qkv[0], qkv[1], qkv[2])
        q = _layernorm(q, q_norm_w, q_norm_b)
        k = _layernorm(k, k_norm_w, k_norm_b)
        attn = jax.nn.softmax(jnp.einsum('bhqd,bhkd->bhqk', q * scale, k), axis=-1)
        o = jnp.einsum('bhqk,bhkd->bhqd', attn, v)
        o = jnp.transpose(o, (0, 2, 1, 3))
        shared_gates = jax.nn.softmax(x @ wg1_w, axis=-1) * SHARED
        w0 = jax.nn.softmax(x @ wg0_w, axis=-1) * 2.0
        shared_gates = w0[..., 0:1] * shared_gates
        routed_gates = w0[..., 1:2] * routed_gates
        masked_gates = jnp.concatenate([shared_gates, routed_gates], axis=-1)
        o = (masked_gates[..., None] * o).reshape(B, N, H * HD)
        return o @ proj_w + proj_b
    h = _L0_tok_ref(x, L0_tok_W, L0_tok_b, L0_tok_class_token, L0_tok_pos_embed)
    h = h + _L0_attn_ref(_layernorm(h, axis=-1), L0_attn_w_q, L0_attn_w_k, L0_attn_w_v, L0_attn_w_o, L0_attn_rel_emb)
    h = h + _L0_ffn_ref(_layernorm(h, axis=-1), L0_ffn_qkv_w, L0_ffn_qkv_b, L0_ffn_q_norm_w, L0_ffn_q_norm_b, L0_ffn_k_norm_w, L0_ffn_k_norm_b, L0_ffn_wg_w, L0_ffn_wg0_w, L0_ffn_wg1_w, L0_ffn_proj_w, L0_ffn_proj_b)
    return h

_drawn_inputs = setup_inputs


def setup_inputs(seed=0):
    import zlib

    import numpy as np

    out = dict(_drawn_inputs(seed))
    spreads = {'L0_tok_b': (0.0, 0.1),
     'L0_ffn_qkv_b': (0.0, 0.1),
     'L0_ffn_q_norm_w': (1.0, 0.6),
     'L0_ffn_q_norm_b': (0.0, 2.0),
     'L0_ffn_k_norm_w': (1.0, 0.6),
     'L0_ffn_k_norm_b': (0.0, 2.0),
     'L0_ffn_proj_b': (0.0, 0.1)}
    factors = {'L0_attn_w_q': 8.0,
     'L0_attn_w_k': 8.0,
     'L0_attn_rel_emb': 8.0,
     'L0_ffn_wg0_w': 6.25,
     'L0_ffn_wg1_w': 8.0}
    for name, (base, spread) in spreads.items():
        noise = np.random.default_rng([zlib.crc32(name.encode()), seed]).standard_normal(out[name].shape)
        drawn = base * np.exp(spread * noise) if base else spread * noise
        out[name] = jnp.asarray(drawn.astype(out[name].dtype))
    for name, factor in factors.items():
        out[name] = (out[name] * factor).astype(out[name].dtype)
    return out
```

```python
from contextlib import ExitStack

import concourse.bass as bass
from concourse import mybir

ALU = mybir.AluOpType
ACT = mybir.ActivationFunctionType
AX = mybir.AxisListType
F32 = mybir.dt.float32
F32R = mybir.dt.float32r

IMAGES, CHANNELS, SIDE = 64, 3, 224
GRID = 14
PATCH = SIDE // GRID
DIM = 192
PATCHES = GRID * GRID
SEQ = PATCHES + 1
AH, AD = 8, 96
FH, FD = 12, 64
SHARED = 2
ROUTED = FH - SHARED
TOPK = 2
MAX_DIST = 100
LN_EPS = 1e-5
FLT_EPS = 1.1920929e-07

TILES = 2
HALF = PATCHES // TILES
ROWS = HALF + 1
COLS = TILES * ROWS
KEYS = (ROWS, HALF)
TILE_AT = (slice(0, ROWS), slice(ROWS, COLS))

PW = PATCH // 2
TOK_K = CHANNELS * PATCH
QK_W = 2 * FH * FD
V_W = FH * FD
GATES_W = 2 + SHARED + ROUTED
W1_W = 3 * AH * AD
W2_W = QK_W + V_W + GATES_W
CHUNK = 512
VCHUNK = 384
HEADS = AH + FH
AG, FG = AH // 2, FH // 2

BANK_ORDER = (
    [("v1", t, c) for t in range(TILES) for c in range(2)]
    + [("qk1", h) for h in range(AH)]
    + [("tok",), ("out",), ("x2t",)]
    + [("qk2", t, c) for t in range(TILES) for c in range(3)]
    + [("gates",)]
    + [("v2", t, c) for t in range(TILES) for c in range(2)]
    + [("ft", 0), ("ft", 1), ("ft", 2), ("x1t",), ("ft", 3), ("ft", 4), ("ft", 5)]
    + [("proj",)]
)
assert len(BANK_ORDER) % 2 == 0
BANK_USES = len(BANK_ORDER) // 2
BANK_USE = {name: n for n, name in enumerate(BANK_ORDER)}

DVE_STEPS = 45


class Steps:

    def __init__(self, sem, base=0):
        self.sem, self.base, self.n = sem, base, 0

    def mark(self, ins):
        ins.then_inc(self.sem, 1)
        self.n += 1

    def value(self):
        return self.base + self.n


def vit_kernel(nc, x, tok_w, tok_b, cls, pos, w_q, w_k, w_v, w_o, rel_emb, qkv_w, qkv_b,
               qn_w, qn_b, kn_w, kn_b, wg, wg0, wg1, proj_w, proj_b, out):
    ext_w = 2 * (SEQ - 1) + 1
    dist_dram = nc.dram_tensor("dist_ext", (AH, SEQ, ext_w), F32, kind="Internal").ap()
    with ExitStack() as ctx:
        def sb(name, shape, dt=F32):
            return ctx.enter_context(nc.sbuf_tensor(name, shape, dt))

        def ps(name, shape):
            return ctx.enter_context(nc.psum_tensor(name, shape, F32))

        def sem(name):
            return ctx.enter_context(nc.semaphore(name))

        ident = sb("ident", [128, 128])
        eps_pow = sb("eps_pow", [128, 2 * FH])
        w1 = [sb(f"w1_{n}", [128, W1_W], F32R) for n in ("hi_a", "lo_a", "hi_c", "lo_c")]
        w2 = [sb(f"w2_{n}", [128, W2_W], F32R) for n in ("hi_a", "lo_a", "hi_c", "lo_c")]
        wtok = sb("wtok", [2 * TOK_K, PW, DIM])
        wo = sb("wo", [AD, AH, DIM])
        wp = sb("wp", [128, FG, DIM])
        dist = sb("dist", [ROWS, TILES, AH, COLS])
        posb = sb("posb", [ROWS, TILES, DIM])
        bqk = sb("bqk", [ROWS, QK_W])
        bv = sb("bv", [ROWS, V_W])
        bproj = sb("bproj", [ROWS, TILES, DIM])
        aff = sb("aff", [128, 4])
        ximg = sb("ximg", [2 * TOK_K, GRID, SIDE])
        h0 = [sb(f"h0_{p}", [ROWS, TILES, DIM]) for p in range(2)]
        h1 = sb("h1", [ROWS, TILES, DIM])
        h1b = sb("h1b", [ROWS, TILES, DIM])
        osb = [sb(f"osb{p}", [ROWS, TILES, DIM]) for p in range(2)]
        xn = sb("xn", [ROWS, TILES, DIM + 64])
        xh = [sb(f"xh{n}", [128, 2, COLS], F32R) for n in (1, 2)]
        xl = [sb(f"xl{n}", [128, COLS], F32R) for n in (1, 2)]
        values = sb("values", [128, 2, TILES * V_W])
        v1, v2 = (values[0:ROWS, n, :].rearrange("p (t e) -> p t e", t=TILES) for n in range(2))
        qkt = [sb(f"qkt{i}", [AD, 2, COLS]) for i in range(2)]
        logits = [sb(f"logits{i}", [ROWS, TILES, COLS]) for i in range(2)]
        prob = [sb(f"prob{i}", [ROWS, TILES, COLS]) for i in range(4)]
        negmax = [sb(f"negmax{i}", [ROWS, 2 * TILES]) for i in range(4)]
        psumr = [sb(f"rowsum{i}", [ROWS, TILES]) for i in range(4)]
        rec = [sb(f"rec{i}", [ROWS, TILES]) for i in range(4)]
        probt = [sb(f"probt{i}", [ROWS, TILES, COLS]) for i in range(2)]
        ctx1 = sb("ctx1", [AD, AH, COLS])
        ctx2 = sb("ctx2", [128, FG, COLS])
        qk2_full = sb("qk2", [128, TILES, QK_W])
        qk2 = qk2_full[0:ROWS, :, :]
        sq_full = sb("sq", [128, QK_W])
        sq = sq_full[0:ROWS, :]
        ss = sb("ss", [ROWS, TILES, 2 * FH])
        qz = [[sb(f"qz{i}{a}", [128, COLS]) for a in range(2)] for i in range(2)]
        kt = [sb(f"kt{i}", [128, COLS]) for i in range(2)]
        bn = sb("bn", [ROWS, TILES, 6])
        mv = sb("mv", [ROWS, TILES, 2])
        var = sb("var", [ROWS, TILES])
        rstd = sb("rstd", [ROWS, TILES])
        gmax = sb("gmax", [ROWS, TILES, 3])
        gsum = sb("gsum", [ROWS, TILES, 3])
        glog = sb("glog", [ROWS, TILES, 4 + 16])
        gexp = sb("gexp", [ROWS, TILES, 4 + 16])
        gtop = sb("gtop", [ROWS, TILES, 8])
        gcut = sb("gcut", [ROWS, TILES, 16])
        gsel = sb("gsel", [ROWS, TILES, ROUTED])
        gden = sb("gden", [ROWS, TILES])
        gate = sb("gate", [ROWS, TILES, FH])
        stage_a = qk2_full[:, :, :].rearrange("p t e -> p (t e)")
        stage_c = values[:, :, :].rearrange("p t e -> p (t e)")
        setup_mean = sb("setup_mean", [128, 2 * FH])
        wtok_scratch = ximg[:, :, :].rearrange("p a b -> p (a b)")[:, 0:4 * PATCH * TOK_K]
        wtok_scratch = wtok_scratch.rearrange("p (s n) -> p s n", s=4)
        wtok_rows, wtok_perm = wtok_scratch[:, 0:2, :], wtok_scratch[:, 2:4, :]
        rel_rows = sq_full[:, :].rearrange("p (t h d) -> p t h d", t=2, h=AH)
        rel_sum = sb("rel_sum", [128, 2, AH])
        ext = sb("ext", [AH, ext_w])

        bank_s = [ps(f"bank_s{i}", [128, 512]) for i in range(2)]
        bank_t = [ps(f"bank_t{i}", [128, 512]) for i in range(2)]
        bank_c = [ps(f"bank_c{i}", [128, 512]) for i in range(2)]
        bank_q = [ps(f"bank_q{i}", [128, 512]) for i in range(2)]

        s_wload = sem("s_wload")
        s_stage1 = sem("s_stage1")
        s_stage2 = sem("s_stage2")
        s_misc = sem("s_misc")
        s_ident = sem("s_ident")
        s_staged = sem("s_staged")
        s_whi = sem("s_whi")
        s_wlo = sem("s_wlo")
        s_wtok_p = sem("s_wtok_p")
        s_wtok_t = sem("s_wtok_t")
        s_wtok_c = sem("s_wtok_c")
        s_rel_t = sem("s_rel_t")
        s_ext = sem("s_ext")
        s_ext_out = sem("s_ext_out")
        s_dist = sem("s_dist")
        s_dve = sem("s_dve")
        s_apart = sem("s_apart")
        s_pool = sem("s_pool")
        s_x = sem("s_x")
        s_q_full = [sem(f"s_q_full{i}") for i in range(2)]
        s_q_free = [sem(f"s_q_free{i}") for i in range(2)]
        s_var = sem("s_var")
        s_rstd = sem("s_rstd")
        s_xn = sem("s_xn")
        s_xhi = sem("s_xhi")
        s_v1 = sem("s_v1")
        s_qkt = sem("s_qkt")
        s_score = sem("s_score")
        s_logit = sem("s_logit")
        s_max = sem("s_max")
        s_exp = sem("s_exp")
        s_rec = sem("s_rec")
        s_prob = sem("s_prob")
        s_pt = sem("s_pt")
        s_pte = [sem("s_pte_act"), sem("s_pte_dve")]
        s_pv = sem("s_pv")
        s_ctx = sem("s_ctx")
        s_h1 = sem("s_h1")
        s_h1b = sem("s_h1b")
        s_qk2 = sem("s_qk2")
        s_sq = sem("s_sq")
        s_ss = sem("s_ss")
        s_qrstd = sem("s_qrstd")
        s_qn = sem("s_qn")
        s_v2 = sem("s_v2")
        s_glog = sem("s_glog")
        s_gexp = sem("s_gexp")
        s_ft = sem("s_ft")
        s_osb = sem("s_osb")
        s_out = [sem(f"s_out{p}") for p in range(2)]

        def ev(img, per_image, n):
            return img * per_image + n + 1

        def before(img, per_image):
            return img * per_image + 1

        def head_ev(img, g):
            return img * HEADS + g + 2

        def pair_ev(img, u):
            return img * (HEADS // 2) + u + 2

        def q_bank(name):
            return bank_q[BANK_USE[name] % 2]

        def q_full(eng, img, name):
            n = BANK_USE[name]
            eng.wait_ge(s_q_full[n % 2], img * BANK_USES + 1 + n // 2 + 1)

        def q_wait_free(eng, img, name):
            n = BANK_USE[name]
            eng.wait_ge(s_q_free[n % 2], img * BANK_USES + 1 + n // 2)

        def q_filled(ins, name):
            ins.then_inc(s_q_full[BANK_USE[name] % 2], 1)

        def q_freed(ins, name):
            ins.then_inc(s_q_free[BANK_USE[name] % 2], 1)

        block = ctx.enter_context(nc.Block())

        x_rows = x.rearrange("n c (i r) w -> n c r i w", r=PATCH)
        N_MISC = 4 + 2 + 2 + TILES + 8 + 2 + AH + FG
        N_ZEROED = 3 + 7 + 4

        @block.sync
        def _(sp):
            def load_w1(dst_rows, src_rows):
                n = src_rows.stop - src_rows.start
                for k, w in enumerate((w_q, w_k, w_v)):
                    for dst, at in dst_rows:
                        o = dst[at:at + n, k * AH * AD:(k + 1) * AH * AD].rearrange("e (h d) -> e h d", h=AH)
                        sp.dma_start(o, w[:, src_rows, :].rearrange("h e d -> e h d")).then_inc(s_stage1, 16)

            load_w1([(stage_a, 0)], slice(0, 128))
            load_w1([(stage_c, 0), (stage_c, 64)], slice(128, DIM))
            for half in range(2):
                sp.dma_start(wtok_rows[:, half, :], tok_w[half * 96:(half + 1) * 96, :]).then_inc(s_wload, 16)
            row = lambda a: a.rearrange("(o n) -> o n", o=1)
            sp.wait_ge(s_ident, N_ZEROED)
            for t in range(TILES):
                sp.dma_start(posb[0:HALF, t, :], pos[1 + t * HALF:1 + (t + 1) * HALF, :]).then_inc(s_misc, 16)
                sp.dma_start(h0[0][0:HALF, t, :], row(tok_b).to_broadcast([HALF, DIM])).then_inc(s_misc, 16)
            sp.dma_start(posb[HALF:ROWS, 0, :], pos[0:1, :]).then_inc(s_misc, 16)
            sp.dma_start(h0[0][HALF:ROWS, 0, :], cls).then_inc(s_misc, 16)
            sp.dma_start(bqk[:, :], row(qkv_b[0:QK_W]).to_broadcast([ROWS, QK_W])).then_inc(s_misc, 16)
            sp.dma_start(bv[:, :], row(qkv_b[QK_W:QK_W + V_W]).to_broadcast([ROWS, V_W])).then_inc(s_misc, 16)
            for t in range(TILES):
                sp.dma_start(bproj[:, t, :], row(proj_b).to_broadcast([ROWS, DIM])).then_inc(s_misc, 16)
            for n, v in enumerate((qn_w, qn_b, kn_w, kn_b)):
                for half in range(2):
                    sp.dma_start(aff[half * 64:half * 64 + 64, n:n + 1],
                                 v.rearrange("(d o) -> d o", o=1)).then_inc(s_misc, 16)
            sp.dma_start(rel_rows[:, 0, :, :],
                         rel_emb[:, 0:128, :, 0].rearrange("h r d -> r h d")).then_inc(s_misc, 16)
            sp.dma_start(rel_rows[0:2 * MAX_DIST - 1 - 128, 1, :, :],
                         rel_emb[:, 128:2 * MAX_DIST - 1, :, 0].rearrange("h r d -> r h d")).then_inc(s_misc, 16)
            for h in range(AH):
                sp.dma_start(wo[:, h, :], w_o[h, :, :]).then_inc(s_misc, 16)
            for g in range(FG):
                sp.dma_start(wp[:, g, :], proj_w[g * 128:(g + 1) * 128, :]).then_inc(s_misc, 16)
            sp.wait_ge(s_wlo, 4)
            for dst, at, a, b in ((stage_a, 0, 0, 128), (stage_c, 0, 128, DIM), (stage_c, 64, 128, DIM)):
                rows = slice(at, at + b - a)
                sp.dma_start(dst[rows, 0:QK_W + V_W], qkv_w[a:b, :]).then_inc(s_stage2, 16)
                g = QK_W + V_W
                sp.dma_start(dst[rows, g:g + 2], wg0[a:b, :]).then_inc(s_stage2, 16)
                sp.dma_start(dst[rows, g + 2:g + 4], wg1[a:b, :]).then_inc(s_stage2, 16)
                sp.dma_start(dst[rows, g + 4:g + 14], wg[a:b, :]).then_inc(s_stage2, 16)
            sp.wait_ge(s_ext, 1)
            sp.dma_start(dist_dram, ext[:, :].unsqueeze(1).to_broadcast([AH, SEQ, ext_w])).then_inc(s_ext_out, 16)
            sp.wait_ge(s_ext_out, 16)
            for rows, t, q0, nq in ((slice(0, HALF), 0, 1, HALF), (slice(HALF, ROWS), 0, 0, 1),
                                    (slice(0, HALF), 1, 1 + HALF, HALF)):
                for at, k0, nk in ((0, 1, HALF), (HALF, 0, 1), (ROWS, 1 + HALF, HALF)):
                    src = bass.AP(dist_dram.tensor, q0 * (ext_w - 1) + k0 + SEQ - 1,
                                 [[ext_w - 1, nq], [SEQ * ext_w, AH], [1, nk]])
                    sp.dma_start(dist[rows, t, :, at:at + nk], src, allow_slow_non_contiguous=nk == 1).then_inc(s_dist, 16)

            def load_x(img):
                for g in range(2):
                    for c in range(CHANNELS):
                        part = slice(g * TOK_K + c * PATCH, g * TOK_K + (c + 1) * PATCH)
                        w = SIDE - g * PW
                        src = x_rows[img, c, :, :, g * PW:SIDE] if isinstance(img, int) else \
                            x_rows[bass.ds(img, 1), c, :, :, g * PW:SIDE].rearrange("n r i w -> (n r) i w")
                        sp.dma_start(ximg[part, :, 0:w], src).then_inc(s_x, 16)

            sp.wait_ge(s_wtok_t, 16)
            load_x(0)
            sp.wait_ge(s_q_full[0], 1)
            load_x(1)

            for p in range(2):
                sp.sem_inc(s_out[p], 16)

            def store(img, it, p):
                sp.wait_ge(s_osb, before(img + 1, 1))
                at = (lambda a, b: out[img, a:b, :]) if isinstance(img, int) else \
                    (lambda a, b: out[bass.ds(img, 1), a:b, :].rearrange("n s e -> (n s) e"))
                sp.dma_start(at(1, ROWS), osb[p][0:HALF, 0, :]).then_inc(s_out[p], 16)
                sp.dma_start(at(0, 1), osb[p][HALF:ROWS, 0, :]).then_inc(s_out[p], 16)
                sp.dma_start(at(ROWS, SEQ), osb[p][0:HALF, 1, :]).then_inc(s_out[p], 16)

            def slot(it, p, nxt):
                img = it * 2 + p
                if nxt is not None:
                    q_full(sp, img, ("tok",))
                    load_x(nxt)
                store(img, it, p)

            with sp.Fori(0, IMAGES // 2 - 1) as it:
                for p in range(2):
                    slot(it, p, it * 2 + (p + 2))
            slot(IMAGES // 2 - 1, 0, 0)
            slot(IMAGES // 2 - 1, 1, None)
            for p in range(2):
                sp.wait_ge(s_out[p], 48 * (IMAGES // 2) + 16)

        @block.tensor
        def _(pe):
            pe.wait_ge(s_ident, N_ZEROED)
            pe.wait_ge(s_wtok_p, 2)
            for half in range(2):
                rows = wtok_perm[:, half, :].rearrange("e (w k) -> e w k", w=PW)
                for w in range(PW):
                    n = half * PW + w
                    if n >= 2:
                        pe.wait_ge(s_wtok_c, n - 1)
                    nc.tensor.transpose(bank_t[n % 2][0:96, 0:96], rows[:, w, :],
                                        ident[0:96, 0:96]).then_inc(s_wtok_t, 1)
            pe.wait_ge(s_dve, 2)
            r1 = 2 * MAX_DIST - 1 - 128
            nc.tensor.transpose(bank_s[0][0:AH, 0:128], rel_sum[:, 0, :], ident[:, :]).then_inc(s_rel_t, 1)
            nc.tensor.transpose(bank_s[1][0:AH, 0:r1], rel_sum[0:r1, 1, :], ident[0:r1, 0:r1]).then_inc(s_rel_t, 1)

            def embed(bank, img):
                pe.wait_ge(s_x, (img + 1) * (2 * CHANNELS * 16))
                for t in range(TILES):
                    for w in range(PW):
                        cols = ximg[:, t * 7:(t + 1) * 7, :].rearrange("k i (j w) -> k i j w", w=PATCH)[:, :, :, w]
                        ins = nc.tensor.matmul(bank[0:HALF, t * DIM:(t + 1) * DIM], cols, wtok[:, w, :],
                                               start=(w == 0), stop=(w == PW - 1))
                return ins

            def transpose_x(bank):
                for t in range(TILES):
                    nc.tensor.transpose(bank[:, t * ROWS:(t + 1) * ROWS], xn[:, t, 0:128], ident[0:ROWS, 0:ROWS])
                    ins = nc.tensor.transpose(bank[:, COLS + t * ROWS:COLS + (t + 1) * ROWS],
                                              xn[:, t, 128:256], ident[0:ROWS, 0:ROWS])
                return ins

            def terms(n, w):
                hi_a, lo_a, hi_c, lo_c = w
                return [(xh[n][:, 0, :], lo_a), (xl[n][:, :], hi_a), (xh[n][:, 1, :], lo_c),
                        (xh[n][:, 1, :], hi_c), (xh[n][:, 0, :], hi_a)]

            def rows_by(bank_out, n, w, t, cols):
                tt = terms(n, w)
                for i, (a, b) in enumerate(tt):
                    ins = nc.tensor.matmul(bank_out, a[:, TILE_AT[t]], b[:, cols], start=(i == 0), stop=(i == len(tt) - 1))
                return ins

            pe.wait_ge(s_wtok_c, 16)
            embed(bank_q[0], 0).then_inc(s_q_full[0], 1)
            pe.wait_ge(s_xn, 1)
            transpose_x(bank_q[1]).then_inc(s_q_full[1], 1)
            pe.wait_ge(s_wlo, 8)
            pe.wait_ge(s_misc, 16 * N_MISC)

            def image(it, p):
                img = it * 2 + p
                pe.wait_ge(s_xhi, ev(img, 2, 0))
                pe.wait_ge(s_xn, ev(img, 4, 1))

                def v1_chunk(t, c):
                    q_wait_free(pe, img, ("v1", t, c))
                    q_filled(rows_by(q_bank(("v1", t, c))[0:ROWS, 0:VCHUNK], 0, w1, t,
                                     slice(2 * AH * AD + c * VCHUNK, 2 * AH * AD + (c + 1) * VCHUNK)), ("v1", t, c))

                def qk1_head(h):
                    q_wait_free(pe, img, ("qk1", h))
                    tt = terms(0, w1)
                    for k in range(2):
                        cols = slice(k * AH * AD + h * AD, k * AH * AD + (h + 1) * AD)
                        for i, (a, b) in enumerate(tt):
                            ins = nc.tensor.matmul(q_bank(("qk1", h))[0:AD, k * COLS:(k + 1) * COLS],
                                                   b[:, cols], a, start=(i == 0), stop=(i == len(tt) - 1))
                    q_filled(ins, ("qk1", h))

                def score(g):
                    bank = bank_s[g % 2]
                    if g in (0, 1):
                        pe.wait_ge(s_exp, before(img, HEADS))
                    elif g < AH + 2:
                        pe.wait_ge(s_logit, ev(img, AH, min(g - 2, AH - 1)))
                    else:
                        pe.wait_ge(s_exp, head_ev(img, g - 2))
                    if g < AH:
                        pe.wait_ge(s_qkt, ev(img, AH, g))
                        q, k = qkt[g % 2][:, 0, :], qkt[g % 2][:, 1, :]
                    else:
                        j = (g - AH) // 2
                        pe.wait_ge(s_ft, ev(img, FG, j))
                        q, k = qz[j % 2][g % 2], kt[j % 2][:, :]
                    for t in range(TILES):
                        ins = nc.tensor.matmul(bank[0:ROWS, t * COLS:(t + 1) * COLS], q[:, TILE_AT[t]], k,
                                               start=True, stop=True)
                    ins.then_inc(s_score, 1)

                def transpose_p(g):
                    pe.wait_ge(s_prob, head_ev(img, g))
                    pe.wait_ge(s_pte[g % 2], pair_ev(img, g // 2 - 1))
                    bank = bank_t[g % 2]
                    for kt_ in range(TILES):
                        for t in range(TILES):
                            ins = nc.tensor.transpose(bank[0:ROWS, kt_ * COLS + t * ROWS:kt_ * COLS + (t + 1) * ROWS],
                                                      prob[g % 4][:, t, TILE_AT[kt_]],
                                                      ident[0:ROWS, 0:ROWS])
                    ins.then_inc(s_pt, 1)

                def mix(g):
                    pe.wait_ge(s_pte[g % 2], pair_ev(img, g // 2))
                    u = g // 2
                    if g % 2 == 0:
                        pe.wait_ge(s_ctx, pair_ev(img, u - 2) if u >= 2 else before(img, HEADS // 2))
                    bank = bank_c[u % 2]
                    if g < AH:
                        o, v = bank[0:AD, (g % 2) * COLS:(g % 2 + 1) * COLS], v1
                        cols = slice(g * AD, (g + 1) * AD)
                        if g == 0:
                            pe.wait_ge(s_v1, ev(img, 4, 3))
                    else:
                        f = g - AH
                        o, v = bank[(f % 2) * 64:(f % 2) * 64 + 64, 0:COLS], v2
                        cols = slice(f * FD, (f + 1) * FD)
                        if f == 0:
                            pe.wait_ge(s_v2, ev(img, 4, 3))
                    for kt_ in range(TILES):
                        n = KEYS[kt_]
                        ins = nc.tensor.matmul(o, v[0:n, kt_, cols], probt[g % 2][0:n, kt_, :],
                                               start=(kt_ == 0), stop=(kt_ == 1))
                    ins.then_inc(s_pv, 1)

                for t in range(TILES):
                    for c in range(2):
                        v1_chunk(t, c)
                for s in range(AH + 4):
                    if s < AH:
                        qk1_head(s)
                    if 1 <= s <= AH:
                        score(s - 1)
                    if s == AH:
                        q_wait_free(pe, img, ("tok",))
                        q_filled(embed(q_bank(("tok",)), img + 1), ("tok",))
                    if 3 <= s < AH + 3:
                        transpose_p(s - 3)
                    if s >= 4:
                        mix(s - 4)
                q_wait_free(pe, img, ("out",))
                pe.wait_ge(s_ctx, pair_ev(img, AG - 1))
                for t in range(TILES):
                    for h in range(AH):
                        ins = nc.tensor.matmul(q_bank(("out",))[0:ROWS, t * DIM:(t + 1) * DIM],
                                               ctx1[:, h, TILE_AT[t]], wo[:, h, :],
                                               start=(h == 0), stop=(h == AH - 1))
                q_filled(ins, ("out",))

                q_wait_free(pe, img, ("x2t",))
                pe.wait_ge(s_xn, ev(img, 4, 2))
                q_filled(transpose_x(q_bank(("x2t",))), ("x2t",))
                pe.wait_ge(s_xhi, ev(img, 2, 1))
                pe.wait_ge(s_xn, ev(img, 4, 3))
                for t in range(TILES):
                    for c in range(3):
                        q_wait_free(pe, img, ("qk2", t, c))
                        q_filled(rows_by(q_bank(("qk2", t, c))[0:ROWS, :], 1, w2, t,
                                         slice(c * CHUNK, (c + 1) * CHUNK)), ("qk2", t, c))
                q_wait_free(pe, img, ("gates",))
                for t in range(TILES):
                    ins = rows_by(q_bank(("gates",))[0:ROWS, t * GATES_W:(t + 1) * GATES_W], 1, w2, t,
                                  slice(QK_W + V_W, W2_W))
                q_filled(ins, ("gates",))
                for t in range(TILES):
                    for c in range(2):
                        q_wait_free(pe, img, ("v2", t, c))
                        q_filled(rows_by(q_bank(("v2", t, c))[0:ROWS, 0:VCHUNK], 1, w2, t,
                                         slice(QK_W + c * VCHUNK, QK_W + (c + 1) * VCHUNK)), ("v2", t, c))

                def turn_qk(j):
                    q_wait_free(pe, img, ("ft", j))
                    bank = q_bank(("ft", j))
                    for k in range(2):
                        for t in range(TILES):
                            if j == 0 and k == 0:
                                pe.wait_ge(s_qn, ev(img, TILES, t))
                            a = k * V_W + j * 128
                            ins = nc.tensor.transpose(bank[:, k * COLS + t * ROWS:k * COLS + (t + 1) * ROWS],
                                                      qk2[:, t, a:a + 128], ident[0:ROWS, 0:ROWS])
                    q_filled(ins, ("ft", j))

                turn_qk(0)
                for s in range(FH + 4):
                    if s % 2 == 0 and s // 2 + 1 < FG:
                        turn_qk(s // 2 + 1)
                    if s == 4:
                        q_wait_free(pe, img, ("x1t",))
                        pe.wait_ge(s_xn, ev(img + 1, 4, 0))
                        q_filled(transpose_x(q_bank(("x1t",))), ("x1t",))
                    if s < FH:
                        score(AH + s)
                    if 3 <= s < FH + 3:
                        transpose_p(AH + s - 3)
                    if s >= 4:
                        mix(AH + s - 4)
                q_wait_free(pe, img, ("proj",))
                pe.wait_ge(s_ctx, pair_ev(img, HEADS // 2 - 1))
                for t in range(TILES):
                    for j in range(FG):
                        ins = nc.tensor.matmul(q_bank(("proj",))[0:ROWS, t * DIM:(t + 1) * DIM],
                                               ctx2[:, j, TILE_AT[t]], wp[:, j, :],
                                               start=(j == 0), stop=(j == FG - 1))
                q_filled(ins, ("proj",))

            pe.wait_ge(s_dist, 9 * 16)
            for s in (s_score, s_pt, s_pv):
                pe.sem_inc(s, 1)
            with pe.Fori(0, IMAGES // 2) as it:
                for p in range(2):
                    image(it, p)

        @block.scalar
        def _(act):
            def split_weights(stage_w, tiles, first, n):
                for i, st in enumerate((stage_a, stage_c)):
                    act.wait_ge(s_staged, first + i + 1)
                    nc.scalar.activation(tiles[2 * i][:, :], st[:, 0:n], ACT.Copy).then_inc(s_whi, 1)

            act.wait_ge(s_wload, 32)
            for half in range(2):
                src = wtok_rows[:, half, :].rearrange("e (cr g w) -> e w g cr", g=2, w=PW)
                for w in range(PW):
                    ins = nc.scalar.activation(wtok_perm[:, half, w * 96:(w + 1) * 96]
                                               .rearrange("e (g cr) -> e g cr", g=2), src[:, w, :, :], ACT.Copy)
                ins.then_inc(s_wtok_p, 1)
            for n in range(16):
                act.wait_ge(s_wtok_t, n + 1)
                half, w = n // PW, n % PW
                nc.scalar.activation(wtok[:, w, half * 96:(half + 1) * 96], bank_t[n % 2][0:96, 0:96],
                                     ACT.Copy).then_inc(s_wtok_c, 1)
            split_weights(None, w1, 0, W1_W)

            def split_hi(n, bank):
                return nc.scalar.activation(xh[n][:, :, :].rearrange("p a n -> p (a n)"), bank[:, 0:2 * COLS], ACT.Copy)

            act.wait_ge(s_q_full[1], 1)
            split_hi(0, bank_q[1]).then_inc(s_xhi, 1)
            split_weights(None, w2, 2, W2_W)

            def image(it, p):
                img = it * 2 + p

                def v_copy(t, c):
                    name = ("v1", t, c)
                    q_full(act, img, name)
                    if t == 0 and c == 0:
                        act.wait_ge(s_pv, before(img, HEADS))
                    ins = nc.scalar.activation(v1[:, t, c * VCHUNK:(c + 1) * VCHUNK], q_bank(name)[0:ROWS, 0:VCHUNK],
                                               ACT.Copy)
                    ins.then_inc(s_v1, 1)
                    q_free_act(name, s_v1, ev(img, 4, t * 2 + c))

                def q_free_act(name, done, value):
                    act.wait_ge(done, value)
                    act.sem_inc(s_q_free[BANK_USE[name] % 2], 1)

                def qk_copy(h):
                    name = ("qk1", h)
                    q_full(act, img, name)
                    act.wait_ge(s_score, head_ev(img, h - 2) if h >= 2 else before(img, HEADS))
                    nc.scalar.activation(qkt[h % 2][:, :, :].rearrange("p a n -> p (a n)"),
                                         q_bank(name)[0:AD, 0:2 * COLS], ACT.Copy).then_inc(s_qkt, 1)
                    q_free_act(name, s_qkt, ev(img, AH, h))

                def exps(g):
                    act.wait_ge(s_max, head_ev(img, g))
                    act.wait_ge(s_pt, head_ev(img, g - 4) if g >= 4 else before(img, HEADS))
                    src = logits[g % 2] if g < AH else None
                    for t in range(TILES):
                        a = src[:, t, 0:SEQ] if g < AH else bank_s[g % 2][0:ROWS, t * COLS:t * COLS + SEQ]
                        ins = nc.scalar.activation(prob[g % 4][:, t, 0:SEQ], a, ACT.Exp,
                                                   bias=negmax[g % 4][:, t:t + 1],
                                                   accum_out=psumr[g % 4][:, t:t + 1])
                    ins.then_inc(s_exp, 1)

                def pt_copy(g):
                    act.wait_ge(s_pt, head_ev(img, g))
                    act.wait_ge(s_pv, head_ev(img, g - 2) if g >= 2 else before(img, HEADS))
                    nc.scalar.activation(probt[g % 2][:, :, :].rearrange("p a n -> p (a n)"),
                                         bank_t[g % 2][0:ROWS, 0:2 * COLS], ACT.Copy).then_inc(s_pte[0], 1)

                def ctx_copy(u):
                    act.wait_ge(s_pv, head_ev(img, 2 * u + 1))
                    if u < AG:
                        nc.scalar.activation(ctx1[:, 2 * u:2 * u + 2, :].rearrange("p a n -> p (a n)"),
                                             bank_c[u % 2][0:AD, 0:2 * COLS], ACT.Copy).then_inc(s_ctx, 1)
                    else:
                        nc.scalar.activation(ctx2[:, u - AG, :], bank_c[u % 2][:, 0:COLS],
                                             ACT.Copy).then_inc(s_ctx, 1)

                for t in range(TILES):
                    for c in range(2):
                        v_copy(t, c)
                for s in range(AH + 5):
                    if s < AH:
                        qk_copy(s)
                    if 1 <= s <= AH:
                        exps(s - 1)
                    if 3 <= s < AH + 3 and (s - 3) % 2 == 0:
                        pt_copy(s - 3)
                    if s >= 5 and (s - 5) % 2 == 1:
                        ctx_copy((s - 5) // 2)
                q_full(act, img, ("x2t",))
                split_hi(1, q_bank(("x2t",))).then_inc(s_xhi, 1)
                for t in range(TILES):
                    act.wait_ge(s_qk2, ev(img, 6, t * 3 + 2))
                    if t == 1:
                        act.wait_ge(s_ss, ev(img, TILES, 0))
                    nc.scalar.activation(sq[:, :], qk2[:, t, :], ACT.Square).then_inc(s_sq, 1)
                act.wait_ge(s_glog, img + 1)
                nc.scalar.activation(gexp[:, :, 0:GATES_W], glog[:, :, 0:GATES_W], ACT.Exp).then_inc(s_gexp, 1)

                def turned(j):
                    name = ("ft", j)
                    q_full(act, img, name)
                    act.wait_ge(s_score, head_ev(img, AH + 2 * (j - 2) + 1) if j >= 2 else head_ev(img, AH - 1))
                    bank = q_bank(name)
                    for a in range(2):
                        r = slice(64 * a, 64 * a + 64)
                        nc.scalar.activation(qz[j % 2][a][r, :], bank[r, 0:COLS], ACT.Identity,
                                             bias=aff[r, 1:2], scale=aff[r, 0:1])
                    nc.scalar.activation(kt[j % 2][:, :], bank[:, COLS:2 * COLS], ACT.Identity,
                                         bias=aff[:, 3:4], scale=aff[:, 2:3]).then_inc(s_ft, 1)
                    q_free_act(name, s_ft, ev(img, FG, j))

                turned(0)
                for s in range(FH + 5):
                    if s % 2 == 0 and s // 2 + 1 < FG:
                        turned(s // 2 + 1)
                    if s == 4:
                        q_full(act, img, ("x1t",))
                        split_hi(0, q_bank(("x1t",))).then_inc(s_xhi, 1)
                    if s < FH:
                        exps(AH + s)
                    if 3 <= s < FH + 3 and (s - 3) % 2 == 0:
                        pt_copy(AH + s - 3)
                    if s >= 5 and (s - 5) % 2 == 1:
                        ctx_copy(AG + (s - 5) // 2)

            for s in (s_exp, s_pte[0], s_ctx):
                act.sem_inc(s, 1)
            with act.Fori(0, IMAGES // 2) as it:
                for p in range(2):
                    image(it, p)

        @block.vector
        def _(dve):
            chain = Steps(s_dve)

            def step(ins):
                chain.mark(ins)
                return ins

            def ready(apart=False):
                dve.wait_ge(s_dve, chain.value())
                if apart:
                    dve.sem_inc(s_apart, 1)

            dve.wait_ge(s_misc, 16 * N_MISC)
            r1 = 2 * MAX_DIST - 1 - 128
            step(nc.vector.reduce_sum(rel_sum[:, 0, :], rel_rows[:, 0, :, :], AX.X))
            step(nc.vector.reduce_sum(rel_sum[0:r1, 1, :], rel_rows[0:r1, 1, :, :], AX.X))
            step(nc.vector.tensor_tensor(posb[:, :, :], posb[:, :, :], h0[0][:, :, :], ALU.add))
            ready()
            step(nc.vector.tensor_copy(h0[0][:, :, :], posb[:, :, :]))
            step(nc.vector.tensor_copy(h0[1][:, :, :], posb[:, :, :]))
            step(nc.vector.tensor_scalar(aff[:, 0:2], aff[:, 0:2], float(FD) ** -0.5, None, ALU.mult))
            first = SEQ - 1 - (MAX_DIST - 1)
            dve.wait_ge(s_rel_t, 2)
            step(nc.vector.memset(ext[:, :], 0.0))
            ready()
            step(nc.vector.tensor_copy(ext[:, first:first + 128], bank_s[0][0:AH, 0:128]))
            step(nc.vector.tensor_copy(ext[:, first + 128:first + 128 + r1], bank_s[1][0:AH, 0:r1]))
            ready()
            step(nc.vector.tensor_scalar(ext[:, 0:first], ext[:, 0:first], ext[:, first:first + 1], None, ALU.add))
            e = first + 2 * MAX_DIST - 1
            step(nc.vector.tensor_scalar(ext[:, e:], ext[:, e:], ext[:, e - 1:e], None, ALU.add))
            ready()
            nc.vector.tensor_copy(ext[:, e:e + 1], ext[:, e + 1:e + 2]).then_inc(s_ext, 1)
            dve.wait_ge(s_stage1, 9 * 16)
            for st in (stage_a, stage_c):
                nc.vector.tensor_scalar(st[:, 0:AH * AD], st[:, 0:AH * AD], float(AD) ** -0.5, None,
                                        ALU.mult).then_inc(s_staged, 1)

            def split_weights(tiles, first, n):
                for i, st in enumerate((stage_a, stage_c)):
                    dve.wait_ge(s_whi, first + i + 1)
                    for half in range(2):
                        cols = slice(half * (n // 2), (half + 1) * (n // 2))
                        nc.vector.tensor_tensor(tiles[2 * i + 1][:, cols], st[:, cols],
                                                tiles[2 * i][:, cols].bitcast(F32), ALU.subtract).then_inc(s_wlo, 1)

            dve.wait_ge(s_staged, 2)
            split_weights(w1, 0, W1_W)

            def normalise(h, img_value):
                for t in range(TILES):
                    step(nc.vector.bn_stats(bn[:, t, :], h[:, t, :]))
                ready(apart=True)
                for t in range(TILES):
                    step(nc.vector.bn_aggr(mv[:, t, :], bn[:, t, :]))
                ready()
                nc.vector.tensor_scalar(var[:, :], mv[:, :, 1], LN_EPS, None, ALU.add).then_inc(s_var, 1)
                dve.wait_ge(s_rstd, img_value)
                for t in range(TILES):
                    step(nc.vector.tensor_scalar(xn[:, t, 0:DIM], h[:, t, :], mv[:, t, 0:1], rstd[:, t:t + 1],
                                                 ALU.subtract, ALU.mult))
                ready()
                nc.vector.tensor_copy(xn[:, :, DIM:], xn[:, :, 128:DIM]).then_inc(s_xn, 1)

            def split_lo(n, bank):
                nc.vector.tensor_tensor(xl[n][:, :], bank[:, 0:COLS], xh[n][:, 0, :].bitcast(F32), ALU.subtract)
                return nc.vector.tensor_tensor(xh[n][64:128, 1, :], bank[64:128, COLS:2 * COLS],
                                               xh[n][64:128, 1, :].bitcast(F32), ALU.subtract)

            def freed(name, done, value):
                dve.wait_ge(done, value)
                dve.sem_inc(s_q_free[BANK_USE[name] % 2], 1)

            dve.wait_ge(s_q_full[0], 1)
            step(nc.vector.tensor_tensor(h0[0][0:HALF, :, :], bank_q[0][0:HALF, 0:TILES * DIM]
                                         .rearrange("p (t e) -> p t e", t=TILES), posb[0:HALF, :, :], ALU.add))
            ready()
            dve.sem_inc(s_q_free[0], 1)
            normalise(h0[0], 1)
            dve.wait_ge(s_xhi, 1)
            split_lo(0, bank_q[1]).then_inc(s_xn, 1)
            dve.wait_ge(s_xn, 2)
            dve.sem_inc(s_q_free[1], 1)

            dve.wait_ge(s_stage2, 12 * 16)
            for i, (st, rows) in enumerate(((stage_a, 128), (stage_c, 128), (bqk, ROWS))):
                view = st[0:rows, 0:QK_W].rearrange("p (h d) -> p h d", d=FD)
                step(nc.vector.reduce_sum(setup_mean[0:rows, :], view, AX.X))
                ready()
                step(nc.vector.tensor_scalar(setup_mean[0:rows, :], setup_mean[0:rows, :], 1.0 / FD, None, ALU.mult))
                ready()
                ins = nc.vector.tensor_tensor(view, view, setup_mean[0:rows, :].unsqueeze(2)
                                              .to_broadcast([rows, 2 * FH, FD]), ALU.subtract)
                if i < 2:
                    ins.then_inc(s_staged, 1)
                    dve.wait_ge(s_staged, 3 + i)
                else:
                    step(ins)
            split_weights(w2, 2, W2_W)
            step(nc.vector.memset(gexp[:, :, 4 + ROUTED:], -1.0))
            step(nc.vector.memset(gtop[:, :, :], -1.0))
            ready()
            dve.wait_ge(s_dist, 9 * 16)
            setup_steps = chain.n

            def image(it, p):
                img = it * 2 + p
                chain.base, chain.n = setup_steps + img * DVE_STEPS, 0

                def maxes(g):
                    dve.wait_ge(s_score, head_ev(img, g))
                    bank = bank_s[g % 2]
                    nm = negmax[g % 4]
                    dve.wait_ge(s_exp, head_ev(img, g - 4) if g >= 4 else before(img, HEADS))
                    if g < AH:
                        dve.wait_ge(s_exp, head_ev(img, g - 2) if g >= 2 else before(img, HEADS))
                        dve.sem_inc(s_apart, 1)
                        for t in range(TILES):
                            ins = nc.vector.tensor_tensor_reduce(
                                logits[g % 2][:, t, 0:SEQ], bank[0:ROWS, t * COLS:t * COLS + SEQ],
                                dist[:, t, g, 0:SEQ], 1.0, -3.0e38, ALU.add, ALU.max, nm[:, 2 + t:3 + t])
                        ins.then_inc(s_logit, 1)
                        dve.wait_ge(s_logit, ev(img, AH, g))
                        nc.vector.tensor_scalar(nm[:, 0:TILES], nm[:, 2:4], -1.0, None, ALU.mult).then_inc(s_max, 1)
                    else:
                        nc.vector.tensor_reduce(nm[:, 0:TILES], bank[0:ROWS, 0:2 * COLS]
                                                .rearrange("p (t k) -> p t k", t=TILES)[:, :, 0:SEQ],
                                                AX.X, ALU.max, negate=True).then_inc(s_max, 1)

                def recip(g):
                    dve.wait_ge(s_exp, head_ev(img, g))
                    dve.wait_ge(s_prob, head_ev(img, g - 4) if g >= 4 else before(img, HEADS))
                    if g < AH:
                        nc.vector.reciprocal(rec[g % 4][:, :], psumr[g % 4][:, :]).then_inc(s_rec, 1)
                    else:
                        step(nc.vector.reciprocal(psumr[g % 4][:, :], psumr[g % 4][:, :]))
                        ready()
                        nc.vector.tensor_tensor(rec[g % 4][:, :], psumr[g % 4][:, :], gate[:, :, g - AH],
                                                ALU.mult).then_inc(s_rec, 1)

                def pt_copy(g):
                    dve.wait_ge(s_pt, head_ev(img, g))
                    dve.wait_ge(s_pv, head_ev(img, g - 2) if g >= 2 else before(img, HEADS))
                    nc.vector.tensor_copy(probt[g % 2][:, :, :].rearrange("p a n -> p (a n)"),
                                          bank_t[g % 2][0:ROWS, 0:2 * COLS]).then_inc(s_pte[1], 1)

                for s in range(AH + 4):
                    if 1 <= s <= AH:
                        maxes(s - 1)
                    if 3 <= s < AH + 3 and (s - 3) % 2 == 1:
                        pt_copy(s - 3)
                    if 1 <= s <= AH:
                        recip(s - 1)
                    if s == AH:
                        q_full(dve, img, ("tok",))
                        step(nc.vector.tensor_tensor(h0[1 - p][0:HALF, :, :], q_bank(("tok",))[0:HALF, 0:TILES * DIM]
                                                     .rearrange("p (t e) -> p t e", t=TILES),
                                                     posb[0:HALF, :, :], ALU.add))
                        freed(("tok",), s_dve, chain.value())
                q_full(dve, img, ("out",))
                dve.wait_ge(s_h1b, before(img, 1))
                nc.vector.tensor_tensor(h1[:, :, :], q_bank(("out",))[0:ROWS, 0:TILES * DIM]
                                        .rearrange("p (t e) -> p t e", t=TILES), h0[p][:, :, :],
                                        ALU.add).then_inc(s_h1, 1)
                freed(("out",), s_h1, img + 1)
                normalise(h1, ev(img, 2, 1))
                dve.wait_ge(s_xhi, ev(img, 2, 1))
                split_lo(1, q_bank(("x2t",))).then_inc(s_xn, 1)
                freed(("x2t",), s_xn, ev(img, 4, 3))

                for t in range(TILES):
                    for c in range(3):
                        name = ("qk2", t, c)
                        q_full(dve, img, name)
                        cols = slice(c * CHUNK, (c + 1) * CHUNK)
                        nc.vector.tensor_tensor(qk2[:, t, cols], q_bank(name)[0:ROWS, :], bqk[:, cols],
                                                ALU.add).then_inc(s_qk2, 1)
                        freed(name, s_qk2, ev(img, 6, t * 3 + c))
                    if t == 1:
                        q_full(dve, img, ("gates",))
                        lg = q_bank(("gates",))[0:ROWS, 0:TILES * GATES_W].rearrange("p (t n) -> p t n", t=TILES)
                        two = lambda a: a[:, :, 0:4].rearrange("p t (s n) -> p t s n", s=2)
                        b2 = lambda a: a[:, :, 0:2].unsqueeze(3).to_broadcast([ROWS, TILES, 2, 2])
                        b10 = lambda a: a.to_broadcast([ROWS, TILES, ROUTED])
                        step(nc.vector.tensor_reduce(gmax[:, :, 0:2], two(lg), AX.X, ALU.max))
                        step(nc.vector.tensor_reduce(gmax[:, :, 2:3], lg[:, :, 4:14], AX.X, ALU.max))
                        ready()
                        step(nc.vector.tensor_tensor(two(glog), two(lg), b2(gmax), ALU.subtract))
                        nc.vector.tensor_tensor(glog[:, :, 4:14], lg[:, :, 4:14], b10(gmax[:, :, 2:3]),
                                                ALU.subtract).then_inc(s_glog, 1)
                        freed(("gates",), s_glog, img + 1)
                    dve.wait_ge(s_sq, ev(img, TILES, t))
                    nc.vector.reduce_sum(ss[:, t, :], sq[:, :].rearrange("p (h d) -> p h d", d=FD),
                                         AX.X).then_inc(s_ss, 1)
                    dve.wait_ge(s_ss, ev(img, TILES, t))
                    nc.vector.tensor_scalar(ss[:, t, :], ss[:, t, :], 1.0 / FD, LN_EPS, ALU.mult,
                                            ALU.add).then_inc(s_var, 1)
                for t in range(TILES):
                    dve.wait_ge(s_qrstd, ev(img, TILES, t))
                    view = qk2[:, t, :].rearrange("p (h d) -> p h d", d=FD)
                    nc.vector.tensor_tensor(view, view, ss[:, t, :].unsqueeze(2).to_broadcast([ROWS, 2 * FH, FD]),
                                            ALU.mult).then_inc(s_qn, 1)
                for t in range(TILES):
                    for c in range(2):
                        name = ("v2", t, c)
                        q_full(dve, img, name)
                        cols = slice(c * VCHUNK, (c + 1) * VCHUNK)
                        nc.vector.tensor_tensor(v2[:, t, cols], q_bank(name)[0:ROWS, 0:VCHUNK], bv[:, cols],
                                                ALU.add).then_inc(s_v2, 1)
                        freed(name, s_v2, ev(img, 4, t * 2 + c))

                def gates():
                    dve.wait_ge(s_gexp, img + 1)
                    ge = gexp
                    step(nc.vector.tensor_reduce(gsum[:, :, 0:2], two(ge), AX.X, ALU.add))
                    step(nc.vector.tensor_reduce(gsum[:, :, 2:3], ge[:, :, 4:14], AX.X, ALU.add))
                    ready()
                    step(nc.vector.reciprocal(gsum[:, :, :], gsum[:, :, :]))
                    ready()
                    step(nc.vector.tensor_tensor(two(glog), two(ge), b2(gsum), ALU.mult))
                    step(nc.vector.tensor_tensor(ge[:, :, 4:14], ge[:, :, 4:14], b10(gsum[:, :, 2:3]), ALU.mult))
                    ready(apart=True)
                    for t in range(TILES):
                        step(nc.vector.max(gtop[:, t, :], ge[:, t, 4:14]))
                    ready()
                    step(nc.vector.memset(gtop[:, :, TOPK:], -1.0))
                    ready(apart=True)
                    for t in range(TILES):
                        step(nc.vector.match_replace(gcut[:, t, :], gtop[:, t, :], ge[:, t, 4:20], -2.0))
                    ready()
                    step(nc.vector.scalar_tensor_tensor(out=gsel[:, :, :], in0=gcut[:, :, 0:ROUTED], scalar=-1.5,
                                                        in1=ge[:, :, 4:14], op0=ALU.is_lt, op1=ALU.mult))
                    ready()
                    step(nc.vector.tensor_reduce(gden[:, :], gsel[:, :, :], AX.X, ALU.add))
                    ready()
                    step(nc.vector.tensor_scalar(gden[:, :], gden[:, :], FLT_EPS, None, ALU.max))
                    ready()
                    step(nc.vector.reciprocal(gden[:, :], gden[:, :]))
                    ready()
                    step(nc.vector.scalar_tensor_tensor(out=gden[:, :], in0=gden[:, :], scalar=2.0 * TOPK,
                                                        in1=glog[:, :, 1], op0=ALU.mult, op1=ALU.mult))
                    step(nc.vector.scalar_tensor_tensor(out=gate[:, :, 0:SHARED], in0=glog[:, :, 2:4],
                                                        scalar=2.0 * SHARED,
                                                        in1=glog[:, :, 0:1].to_broadcast([ROWS, TILES, SHARED]),
                                                        op0=ALU.mult, op1=ALU.mult))
                    ready()
                    step(nc.vector.tensor_tensor(gate[:, :, SHARED:], gsel[:, :, :],
                                                 gden[:, :].unsqueeze(2).to_broadcast([ROWS, TILES, ROUTED]),
                                                 ALU.mult))
                    ready()

                gates()
                for s in range(FH + 4):
                    if s == 2:
                        normalise(h0[1 - p], ev(img + 1, 2, 0))
                    if s < FH:
                        maxes(AH + s)
                    if s == 4:
                        dve.wait_ge(s_xhi, ev(img + 1, 2, 0))
                        split_lo(0, q_bank(("x1t",))).then_inc(s_xn, 1)
                        freed(("x1t",), s_xn, ev(img + 1, 4, 1))
                    if 3 <= s < FH + 3 and (s - 3) % 2 == 1:
                        pt_copy(AH + s - 3)
                    if s < FH:
                        recip(AH + s)
                q_full(dve, img, ("proj",))
                dve.wait_ge(s_out[p], it * 48 + 16)
                dve.wait_ge(s_h1b, before(img + 1, 1))
                nc.vector.tensor_tensor(osb[p][:, :, :], q_bank(("proj",))[0:ROWS, 0:TILES * DIM]
                                        .rearrange("p (t e) -> p t e", t=TILES), h1b[:, :, :],
                                        ALU.add).then_inc(s_osb, 1)
                freed(("proj",), s_osb, before(img + 1, 1))
                assert chain.n == DVE_STEPS, chain.n

            for s in (s_max, s_rec, s_pte[1], s_osb):
                dve.sem_inc(s, 1)
            with dve.Fori(0, IMAGES // 2) as it:
                for p in range(2):
                    image(it, p)

        @block.gpsimd
        def _(pool):
            nc.gpsimd.memset(ident[:, :], 0.0).then_inc(s_ident, 1)
            nc.gpsimd.memset(eps_pow[:, :], -0.5).then_inc(s_ident, 1)
            pool.wait_ge(s_ident, 2)
            nc.gpsimd.affine_select(out=ident[:, :], in_=ident[:, :], compare_op=ALU.not_equal, fill=1.0,
                                    base=0, pattern=[[-1, 128]], channel_multiplier=1).then_inc(s_ident, 1)
            zeros = [posb[96:ROWS, 1, :], h0[0][96:ROWS, 1, :], dist[:, 1, :, :]]
            zeros += [qz[i][a][64 * (1 - a):64 * (2 - a), :] for i in range(2) for a in range(2)]
            zeros += [pr[:, :, SEQ:COLS] for pr in prob]
            for n, z in enumerate(zeros):
                pool.wait_ge(s_ident, 3 + n)
                nc.gpsimd.memset(z, 0.0).then_inc(s_ident, 1)
            pool.wait_ge(s_ident, N_ZEROED)

            def rsqrt(value, done, a, b, n):
                pool.wait_ge(s_var, value)
                nc.gpsimd.tensor_tensor(b, a, eps_pow[0:ROWS, 0:n], ALU.pow).then_inc(done, 1)

            rsqrt(1, s_rstd, var[:, :], rstd[:, :], TILES)

            def image(it, p):
                img = it * 2 + p

                def scale(g):
                    pool.wait_ge(s_rec, head_ev(img, g))
                    pr = prob[g % 4][:, :, 0:SEQ]
                    nc.gpsimd.tensor_tensor(pr, pr, rec[g % 4][:, :].unsqueeze(2).to_broadcast([ROWS, TILES, SEQ]),
                                            ALU.mult).then_inc(s_prob, 1)

                for g in range(AH):
                    scale(g)
                rsqrt(ev(img, 4, 1), s_rstd, var[:, :], rstd[:, :], TILES)
                pool.wait_ge(s_h1, img + 1)
                pool.wait_ge(s_osb, before(img, 1))
                nc.gpsimd.tensor_tensor(h1b[:, :, :], h1[:, :, :], bproj[:, :, :], ALU.add).then_inc(s_h1b, 1)
                for t in range(TILES):
                    rsqrt(ev(img, 4, 2 + t), s_qrstd, ss[:, t, :], ss[:, t, :], 2 * FH)
                for f in range(FH):
                    if f == 2:
                        rsqrt(ev(img, 4, 4), s_rstd, var[:, :], rstd[:, :], TILES)
                    scale(AH + f)

            for s in (s_prob, s_h1b):
                pool.sem_inc(s, 1)
            with pool.Fori(0, IMAGES // 2) as it:
                for p in range(2):
                    image(it, p)


_INS = ["x", "L0_tok_W", "L0_tok_b", "L0_tok_class_token", "L0_tok_pos_embed", "L0_attn_w_q", "L0_attn_w_k",
        "L0_attn_w_v", "L0_attn_w_o", "L0_attn_rel_emb", "L0_ffn_qkv_w", "L0_ffn_qkv_b", "L0_ffn_q_norm_w",
        "L0_ffn_q_norm_b", "L0_ffn_k_norm_w", "L0_ffn_k_norm_b", "L0_ffn_wg_w", "L0_ffn_wg0_w", "L0_ffn_wg1_w",
        "L0_ffn_proj_w", "L0_ffn_proj_b"]
_OUTS = [((IMAGES, SEQ, DIM), "float32")]


def kernel(**inputs):
    import numpy as _np
    import concourse.bacc as _bacc
    from concourse import mybir as _mybir
    from concourse.bass_utils import run_bass_kernel_spmd as _run

    nc = _bacc.Bacc("TRN2", target_bir_lowering=False, num_devices=1)
    arrays, args = {}, []
    for name in _INS:
        a = _np.ascontiguousarray(inputs[name])
        arrays[f"in_{name}_dram"] = a
        args.append(nc.dram_tensor(f"in_{name}_dram", a.shape, _mybir.dt.from_np(a.dtype), kind="ExternalInput").ap())
    for i, (shape, dtype) in enumerate(_OUTS):
        dt = _mybir.dt.from_np(_np.dtype(dtype))
        args.append(nc.dram_tensor(f"out_{i}_dram", shape, dt, kind="ExternalOutput").ap())
    vit_kernel(nc, *args)
    r = _run(nc, [arrays], core_ids=[0])
    got = tuple(r.results[0][f"out_{i}_dram"] for i in range(len(_OUTS)))
    return got[0]
```

```python
from contextlib import ExitStack

import concourse.bass as bass
from concourse import mybir

ALU = mybir.AluOpType
ACT = mybir.ActivationFunctionType
AX = mybir.AxisListType
F32 = mybir.dt.float32
F32R = mybir.dt.float32r

IMAGES, CHANNELS, SIDE = 64, 3, 224
GRID = 14
PATCH = SIDE // GRID
DIM = 192
PATCHES = GRID * GRID
SEQ = PATCHES + 1
AH, AD = 8, 96
FH, FD = 12, 64
SHARED = 2
ROUTED = FH - SHARED
TOPK = 2
MAX_DIST = 100
LN_EPS = 1e-5
FLT_EPS = 1.1920929e-07

TILES = 2
HALF = PATCHES // TILES
ROWS = HALF + 1
COLS = TILES * ROWS
KEYS = (ROWS, HALF)
TILE_AT = (slice(0, ROWS), slice(ROWS, COLS))

PW = PATCH // 2
TOK_K = CHANNELS * PATCH
QK_W = 2 * FH * FD
V_W = FH * FD
GATES_W = 2 + SHARED + ROUTED
W1_W = 3 * AH * AD
W2_W = QK_W + V_W + GATES_W
CHUNK = 512
VCHUNK = 384
HEADS = AH + FH
AG, FG = AH // 2, FH // 2

LAG = 3
FILL = {
    0: [("qk2", 0, 1), ("qk2", 0, 2)], 1: [("qk2", 1, 0)], 2: [("qk2", 1, 1)], 3: [("qk2", 1, 2)],
    4: [("v2", 0, 1)], 5: [("v2", 1, 1)], 6: [("tok", 0)], 7: [("tok", 1)], 8: [("proj", 0)],
    9: [("v2", 0, 0)], 10: [("v2", 1, 0)], 12: [("proj", 1)], 13: [("out", 0)], 14: [("out", 1)],
    15: [("v1", 0, 0)], 16: [("v1", 0, 1)], 17: [("v1", 1, 0)], 18: [("v1", 1, 1)], 19: [("qk2", 0, 0)],
}
EARLY = [("qk2", 0, 0)]
PREP = {s: ("qk1", s + 1) for s in range(AH - 1)}
PREP |= {AH - 1 + 2 * j: ("ft", j) for j in range(FG)}
PREP |= {10: ("x1t",), 16: ("x2t",), HEADS - 1: ("qk1", 0)}
BANK_ORDER = [u for s in range(HEADS) for u in FILL.get(s, []) + ([PREP[s]] if s in PREP else [])]
assert len(BANK_ORDER) % 2 == 0
BANK_USES = len(BANK_ORDER) // 2
BANK_USE = {name: n for n, name in enumerate(BANK_ORDER)}

V2_ORDER = [name[1:] for name in BANK_ORDER if name[0] == "v2"]

DVE_STEPS = 50


class Turn:

    def __init__(self, k, parity, half, att, ffn, tok, proj, before):
        self.k, self.p, self.half = k, parity, half
        self.att, self.ffn, self.tok, self.proj = att, ffn, tok, proj
        self.before = before

    def has(self, name):
        if name[0] in ("tok", "x1t", "v1") or name == ("qk1", 0):
            return self.tok
        if name[0] in ("qk1", "out", "x2t") or name in EARLY:
            return self.att
        return self.proj if name[0] == "proj" else self.ffn

    def head(self, g):
        if g < 0:
            return self.before.head(g + HEADS) if self.before else None
        return self.att if g < AH else self.ffn


def turns_before():
    t = Turn(-1, 1, 0, False, False, True, False, None)
    yield t
    t = Turn(0, 0, 0, True, False, True, False, t)
    yield t
    yield Turn(1, 1, 0, True, True, True, False, t)


def loop_turn(it, p):
    full = Turn(None, None, None, True, True, True, True, None)
    return Turn(it * 2 + (2 + p), p, it + 1, True, True, True, True, full)


LOOPS = (IMAGES - 4) // 2


def turns_after():
    t = Turn(None, None, None, True, True, True, True, None)
    for k in range(2 + 2 * LOOPS, IMAGES + 2):
        t = Turn(k, k % 2, k // 2, k < IMAGES, k <= IMAGES, k < IMAGES - 1, True, t)
        yield t


LAST_STEP = 12


def steps_of(t):
    last = isinstance(t.k, int) and t.k == IMAGES + 1
    return range(LAST_STEP + 1 if last else HEADS)


class Steps:

    def __init__(self, sem, base=0):
        self.sem, self.base, self.n = sem, base, 0

    def mark(self, ins):
        ins.then_inc(self.sem, 1)
        self.n += 1

    def value(self):
        return self.base + self.n


def vit_kernel(nc, x, tok_w, tok_b, cls, pos, w_q, w_k, w_v, w_o, rel_emb, qkv_w, qkv_b,
               qn_w, qn_b, kn_w, kn_b, wg, wg0, wg1, proj_w, proj_b, out):
    ext_w = 2 * (SEQ - 1) + 1
    dist_dram = nc.dram_tensor("dist_ext", (AH, SEQ, ext_w), F32, kind="Internal").ap()
    with ExitStack() as ctx:
        def sb(name, shape, dt=F32):
            return ctx.enter_context(nc.sbuf_tensor(name, shape, dt))

        def ps(name, shape):
            return ctx.enter_context(nc.psum_tensor(name, shape, F32))

        def sem(name):
            return ctx.enter_context(nc.semaphore(name))

        ident = sb("ident", [128, 128])
        eps_pow = sb("eps_pow", [128, 2 * FH])
        w1 = [sb(f"w1_{n}", [128, W1_W], F32R) for n in ("hi_a", "lo_a", "hi_c", "lo_c")]
        w2 = [sb(f"w2_{n}", [128, W2_W], F32R) for n in ("hi_a", "lo_a", "hi_c", "lo_c")]
        wtok = sb("wtok", [2 * TOK_K, PW, DIM])
        wo = sb("wo", [AD, AH, DIM])
        wp = sb("wp", [128, FG, DIM])
        dist = sb("dist", [ROWS, TILES, AH, COLS])
        posb = sb("posb", [ROWS, TILES, DIM])
        bqk = sb("bqk", [ROWS, QK_W])
        bv = sb("bv", [ROWS, V_W])
        bproj = sb("bproj", [ROWS, DIM])
        aff = sb("aff", [128, 4])
        ximg = sb("ximg", [2 * TOK_K, GRID, SIDE])
        h0 = [sb(f"h0_{p}", [ROWS, TILES, DIM]) for p in range(2)]
        h1 = sb("h1", [ROWS, TILES, DIM])
        h1b = [sb(f"h1b{p}", [ROWS, TILES, DIM]) for p in range(2)]
        osb = [sb(f"osb{p}", [ROWS, TILES, DIM]) for p in range(2)]
        xn = [sb(f"xn{n}", [ROWS, TILES, DIM + 64]) for n in (1, 2)]
        xh = [sb(f"xh{n}", [128, 2, COLS], F32R) for n in (1, 2)]
        xl = [sb(f"xl{n}", [128, COLS], F32R) for n in (1, 2)]
        values = sb("values", [128, 2, TILES * V_W])
        v1, v2 = (values[0:ROWS, n, :].rearrange("p (t e) -> p t e", t=TILES) for n in range(2))
        qkt = [sb(f"qkt{i}", [AD, 2, COLS]) for i in range(2)]
        logits = [sb(f"logits{i}", [ROWS, TILES, COLS]) for i in range(2)]
        prob = [sb(f"prob{i}", [ROWS, TILES, COLS]) for i in range(4)]
        negmax = [sb(f"negmax{i}", [ROWS, 2 * TILES]) for i in range(4)]
        psumr = [sb(f"rowsum{i}", [ROWS, TILES]) for i in range(4)]
        rec = [sb(f"rec{i}", [ROWS, TILES]) for i in range(4)]
        probt = [sb(f"probt{i}", [ROWS, TILES, COLS]) for i in range(2)]
        ctx1 = sb("ctx1", [AD, AH, COLS])
        ctx2 = sb("ctx2", [128, FG, COLS])
        qk2_full = sb("qk2", [128, TILES, QK_W])
        qk2 = qk2_full[0:ROWS, :, :]
        sq_full = sb("sq", [128, QK_W])
        sq = sq_full[0:ROWS, :]
        ss = sb("ss", [ROWS, TILES, 2 * FH])
        qz = [[sb(f"qz{i}{a}", [128, COLS]) for a in range(2)] for i in range(2)]
        kt = [sb(f"kt{i}", [128, COLS]) for i in range(2)]
        bn = [sb(f"bn{n}", [ROWS, TILES, 6]) for n in (1, 2)]
        mv = [sb(f"mv{n}", [ROWS, TILES, 2]) for n in (1, 2)]
        var = [sb(f"var{n}", [ROWS, TILES]) for n in (1, 2)]
        rstd = [sb(f"rstd{n}", [ROWS, TILES]) for n in (1, 2)]
        gmax = sb("gmax", [ROWS, TILES, 3])
        gsum = sb("gsum", [ROWS, TILES, 3])
        glog = sb("glog", [ROWS, TILES, 4 + 16])
        gexp = sb("gexp", [ROWS, TILES, 4 + 16])
        gtop = sb("gtop", [ROWS, TILES, 8])
        gcut = sb("gcut", [ROWS, TILES, 16])
        gsel = sb("gsel", [ROWS, TILES, ROUTED])
        gden = sb("gden", [ROWS, TILES])
        gate = sb("gate", [ROWS, TILES, FH])
        stage_a = qk2_full[:, :, :].rearrange("p t e -> p (t e)")
        stage_c = values[:, :, :].rearrange("p t e -> p (t e)")
        setup_mean = sb("setup_mean", [128, 2 * FH])
        wtok_scratch = ximg[:, :, :].rearrange("p a b -> p (a b)")[:, 0:4 * PATCH * TOK_K]
        wtok_scratch = wtok_scratch.rearrange("p (s n) -> p s n", s=4)
        wtok_rows, wtok_perm = wtok_scratch[:, 0:2, :], wtok_scratch[:, 2:4, :]
        rel_rows = sq_full[:, :].rearrange("p (t h d) -> p t h d", t=2, h=AH)
        rel_sum = sb("rel_sum", [128, 2, AH])
        ext = probt[0][0:AH, :, :].rearrange("p t k -> p (t k)")[:, 0:ext_w]

        bank_s = [ps(f"bank_s{i}", [128, 512]) for i in range(2)]
        bank_t = [ps(f"bank_t{i}", [128, 512]) for i in range(2)]
        bank_c = [ps(f"bank_c{i}", [128, 512]) for i in range(2)]
        bank_q = [ps(f"bank_q{i}", [128, 512]) for i in range(2)]

        s_wload = sem("s_wload")
        s_stage1 = sem("s_stage1")
        s_stage2 = sem("s_stage2")
        s_misc = sem("s_misc")
        s_ident = sem("s_ident")
        s_staged = sem("s_staged")
        s_whi = sem("s_whi")
        s_wlo = sem("s_wlo")
        s_wtok_p = sem("s_wtok_p")
        s_wtok_t = sem("s_wtok_t")
        s_wtok_c = sem("s_wtok_c")
        s_rel_t = sem("s_rel_t")
        s_ext = sem("s_ext")
        s_ext_out = sem("s_ext_out")
        s_dist = sem("s_dist")
        s_dve = sem("s_dve")
        s_apart = sem("s_apart")
        s_pool = sem("s_pool")
        s_x = sem("s_x")
        s_q_full = [sem(f"s_q_full{i}") for i in range(2)]
        s_q_free = [sem(f"s_q_free{i}") for i in range(2)]
        s_var, s_rstd, s_xn, s_xhi, s_xlo = (
            [sem(f"s_{what}{n}") for n in (1, 2)] for what in ("var", "rstd", "xn", "xhi", "xlo"))
        s_qvar = sem("s_qvar")
        s_v1 = sem("s_v1")
        s_qkt = sem("s_qkt")
        s_score = sem("s_score")
        s_logit = sem("s_logit")
        s_max = sem("s_max")
        s_exp = sem("s_exp")
        s_rec = sem("s_rec")
        s_prob = sem("s_prob")
        s_pt = sem("s_pt")
        s_pte = [sem("s_pte_act"), sem("s_pte_dve")]
        s_pv = sem("s_pv")
        s_ctx = sem("s_ctx")
        s_h1 = sem("s_h1")
        s_h1b = sem("s_h1b")
        s_qk2 = sem("s_qk2")
        s_sq = sem("s_sq")
        s_ss = sem("s_ss")
        s_qrstd = sem("s_qrstd")
        s_qn = sem("s_qn")
        s_v2 = sem("s_v2")
        s_glog = sem("s_glog")
        s_gexp = sem("s_gexp")
        s_ft = sem("s_ft")
        s_fk = sem("s_fk")
        s_osb = sem("s_osb")
        s_out = [sem(f"s_out{p}") for p in range(2)]

        def ev(img, per_image, n):
            return img * per_image + n + 1

        def head_ev(t, g):
            return (t.k + 1) * HEADS + (g + 2)

        def pair_ev(t, u):
            return (t.k + 1) * (HEADS // 2) + (u + 2)

        def pass_over(eng, sem_, value):
            eng.wait_ge(sem_, value - 1)
            eng.sem_inc(sem_, 1)

        def q_bank(name):
            return bank_q[BANK_USE[name] % 2]

        def q_full(eng, t, name):
            n = BANK_USE[name]
            eng.wait_ge(s_q_full[n % 2], (t.k + 1) * BANK_USES + (n // 2 + 1))

        def q_wait_free(eng, t, name):
            n = BANK_USE[name]
            value = (t.k + 1) * BANK_USES + n // 2
            if not isinstance(value, int) or value > 0:
                eng.wait_ge(s_q_free[n % 2], value)

        def q_filled(ins, name):
            ins.then_inc(s_q_full[BANK_USE[name] % 2], 1)

        def q_free(eng, name, done, value):
            eng.wait_ge(done, value)
            eng.sem_inc(s_q_free[BANK_USE[name] % 2], 1)

        block = ctx.enter_context(nc.Block())

        x_rows = x.rearrange("n c (i r) w -> n c r i w", r=PATCH)
        N_MISC = 4 + 2 + 2 + 1 + 8 + 2 + AH + FG
        N_ZEROED = 3 + 7 + 4

        @block.sync
        def _(sp):
            def load_w1(dst_rows, src_rows):
                n = src_rows.stop - src_rows.start
                for k, w in enumerate((w_q, w_k, w_v)):
                    for dst, at in dst_rows:
                        o = dst[at:at + n, k * AH * AD:(k + 1) * AH * AD].rearrange("e (h d) -> e h d", h=AH)
                        sp.dma_start(o, w[:, src_rows, :].rearrange("h e d -> e h d")).then_inc(s_stage1, 16)

            load_w1([(stage_a, 0)], slice(0, 128))
            load_w1([(stage_c, 0), (stage_c, 64)], slice(128, DIM))
            for half in range(2):
                sp.dma_start(wtok_rows[:, half, :], tok_w[half * 96:(half + 1) * 96, :]).then_inc(s_wload, 16)
            row = lambda a: a.rearrange("(o n) -> o n", o=1)
            sp.wait_ge(s_ident, N_ZEROED)
            for t in range(TILES):
                sp.dma_start(posb[0:HALF, t, :], pos[1 + t * HALF:1 + (t + 1) * HALF, :]).then_inc(s_misc, 16)
                sp.dma_start(h0[0][0:HALF, t, :], row(tok_b).to_broadcast([HALF, DIM])).then_inc(s_misc, 16)
            sp.dma_start(posb[HALF:ROWS, 0, :], pos[0:1, :]).then_inc(s_misc, 16)
            sp.dma_start(h0[0][HALF:ROWS, 0, :], cls).then_inc(s_misc, 16)
            sp.dma_start(bqk[:, :], row(qkv_b[0:QK_W]).to_broadcast([ROWS, QK_W])).then_inc(s_misc, 16)
            sp.dma_start(bv[:, :], row(qkv_b[QK_W:QK_W + V_W]).to_broadcast([ROWS, V_W])).then_inc(s_misc, 16)
            sp.dma_start(bproj[:, :], row(proj_b).to_broadcast([ROWS, DIM])).then_inc(s_misc, 16)
            for n, v in enumerate((qn_w, qn_b, kn_w, kn_b)):
                for half in range(2):
                    sp.dma_start(aff[half * 64:half * 64 + 64, n:n + 1],
                                 v.rearrange("(d o) -> d o", o=1)).then_inc(s_misc, 16)
            sp.dma_start(rel_rows[:, 0, :, :],
                         rel_emb[:, 0:128, :, 0].rearrange("h r d -> r h d")).then_inc(s_misc, 16)
            sp.dma_start(rel_rows[0:2 * MAX_DIST - 1 - 128, 1, :, :],
                         rel_emb[:, 128:2 * MAX_DIST - 1, :, 0].rearrange("h r d -> r h d")).then_inc(s_misc, 16)
            for h in range(AH):
                sp.dma_start(wo[:, h, :], w_o[h, :, :]).then_inc(s_misc, 16)
            for g in range(FG):
                sp.dma_start(wp[:, g, :], proj_w[g * 128:(g + 1) * 128, :]).then_inc(s_misc, 16)
            sp.wait_ge(s_wlo, 4)
            for dst, at, a, b in ((stage_a, 0, 0, 128), (stage_c, 0, 128, DIM), (stage_c, 64, 128, DIM)):
                rows = slice(at, at + b - a)
                sp.dma_start(dst[rows, 0:QK_W + V_W], qkv_w[a:b, :]).then_inc(s_stage2, 16)
                g = QK_W + V_W
                sp.dma_start(dst[rows, g:g + 2], wg0[a:b, :]).then_inc(s_stage2, 16)
                sp.dma_start(dst[rows, g + 2:g + 4], wg1[a:b, :]).then_inc(s_stage2, 16)
                sp.dma_start(dst[rows, g + 4:g + 14], wg[a:b, :]).then_inc(s_stage2, 16)
            sp.wait_ge(s_ext, 1)
            sp.dma_start(dist_dram, ext[:, :].unsqueeze(1).to_broadcast([AH, SEQ, ext_w])).then_inc(s_ext_out, 16)
            sp.wait_ge(s_ext_out, 16)
            for rows, t, q0, nq in ((slice(0, HALF), 0, 1, HALF), (slice(HALF, ROWS), 0, 0, 1),
                                    (slice(0, HALF), 1, 1 + HALF, HALF)):
                for at, k0, nk in ((0, 1, HALF), (HALF, 0, 1), (ROWS, 1 + HALF, HALF)):
                    src = bass.AP(dist_dram.tensor, q0 * (ext_w - 1) + k0 + SEQ - 1,
                                 [[ext_w - 1, nq], [SEQ * ext_w, AH], [1, nk]])
                    sp.dma_start(dist[rows, t, :, at:at + nk], src, allow_slow_non_contiguous=nk == 1).then_inc(s_dist, 16)

            def load_x(img):
                for g in range(2):
                    for c in range(CHANNELS):
                        part = slice(g * TOK_K + c * PATCH, g * TOK_K + (c + 1) * PATCH)
                        w = SIDE - g * PW
                        src = x_rows[img, c, :, :, g * PW:SIDE] if isinstance(img, int) else \
                            x_rows[bass.ds(img, 1), c, :, :, g * PW:SIDE].rearrange("n r i w -> (n r) i w")
                        sp.dma_start(ximg[part, :, 0:w], src).then_inc(s_x, 16)

            sp.wait_ge(s_wtok_t, 16)
            load_x(0)
            for p in range(2):
                sp.sem_inc(s_out[p], 16)

            def turn(t):
                if t.proj:
                    img = t.k - 2
                    sp.wait_ge(s_osb, ev(img, TILES, 1) + 1)
                    at = (lambda a, b: out[img, a:b, :]) if isinstance(img, int) else \
                        (lambda a, b: out[bass.ds(img, 1), a:b, :].rearrange("n s e -> (n s) e"))
                    o = osb[t.p]
                    sp.dma_start(at(1, ROWS), o[0:HALF, 0, :]).then_inc(s_out[t.p], 16)
                    sp.dma_start(at(0, 1), o[HALF:ROWS, 0, :]).then_inc(s_out[t.p], 16)
                    sp.dma_start(at(ROWS, SEQ), o[0:HALF, 1, :]).then_inc(s_out[t.p], 16)
                if t.tok and not (isinstance(t.k, int) and t.k + 2 >= IMAGES):
                    q_full(sp, t, ("tok", 1))
                    load_x(t.k + 2)

            for t in turns_before():
                turn(t)
            with sp.Fori(0, LOOPS) as it:
                for p in range(2):
                    turn(loop_turn(it, p))
            for t in turns_after():
                turn(t)
            for p in range(2):
                sp.wait_ge(s_out[p], 48 * (IMAGES // 2) + 16)

        @block.tensor
        def _(pe):
            pe.wait_ge(s_ident, N_ZEROED)
            pe.wait_ge(s_wtok_p, 2)
            for half in range(2):
                rows = wtok_perm[:, half, :].rearrange("e (w k) -> e w k", w=PW)
                for w in range(PW):
                    n = half * PW + w
                    if n >= 2:
                        pe.wait_ge(s_wtok_c, n - 1)
                    nc.tensor.transpose(bank_t[n % 2][0:96, 0:96], rows[:, w, :],
                                        ident[0:96, 0:96]).then_inc(s_wtok_t, 1)
            pe.wait_ge(s_dve, 2)
            r1 = 2 * MAX_DIST - 1 - 128
            nc.tensor.transpose(bank_s[0][0:AH, 0:128], rel_sum[:, 0, :], ident[:, :]).then_inc(s_rel_t, 1)
            nc.tensor.transpose(bank_s[1][0:AH, 0:r1], rel_sum[0:r1, 1, :], ident[0:r1, 0:r1]).then_inc(s_rel_t, 1)

            def embed(bank, r):
                for w in range(PW):
                    cols = ximg[:, r * 7:(r + 1) * 7, :].rearrange("k i (j w) -> k i j w", w=PATCH)[:, :, :, w]
                    ins = nc.tensor.matmul(bank[0:HALF, 0:DIM], cols, wtok[:, w, :],
                                           start=(w == 0), stop=(w == PW - 1))
                return ins

            def transpose_x(bank, n):
                for t in range(TILES):
                    nc.tensor.transpose(bank[:, t * ROWS:(t + 1) * ROWS], xn[n][:, t, 0:128], ident[0:ROWS, 0:ROWS])
                    ins = nc.tensor.transpose(bank[:, COLS + t * ROWS:COLS + (t + 1) * ROWS],
                                              xn[n][:, t, 128:256], ident[0:ROWS, 0:ROWS])
                return ins

            def terms(n, w):
                hi_a, lo_a, hi_c, lo_c = w
                return [(xh[n][:, 0, :], lo_a), (xl[n][:, :], hi_a), (xh[n][:, 1, :], lo_c),
                        (xh[n][:, 1, :], hi_c), (xh[n][:, 0, :], hi_a)]

            def rows_by(bank_out, n, w, t, cols):
                tt = terms(n, w)
                for i, (a, b) in enumerate(tt):
                    ins = nc.tensor.matmul(bank_out, a[:, TILE_AT[t]], b[:, cols], start=(i == 0), stop=(i == len(tt) - 1))
                return ins

            pe.wait_ge(s_wtok_c, 16)

            def fill(t, name):
                q_wait_free(pe, t, name)
                bank = q_bank(name)
                if name[0] == "tok":
                    if name[1] == 0:
                        pe.wait_ge(s_x, (t.k + 2) * (2 * CHANNELS * 16))
                    ins = embed(bank, name[1])
                elif name[0] == "x1t":
                    pe.wait_ge(s_xn[0], t.k + 2)
                    ins = transpose_x(bank, 0)
                elif name[0] == "x2t":
                    pe.wait_ge(s_xn[1], t.k + 1)
                    ins = transpose_x(bank, 1)
                elif name[0] == "v1":
                    _, r, c = name
                    if (r, c) == (0, 0):
                        pe.wait_ge(s_xlo[0], t.k + 2)
                    ins = rows_by(bank[0:ROWS, 0:VCHUNK], 0, w1, r,
                                  slice(2 * AH * AD + c * VCHUNK, 2 * AH * AD + (c + 1) * VCHUNK))
                elif name[0] == "qk2":
                    _, r, c = name
                    if (r, c) == (0, 0):
                        pe.wait_ge(s_xlo[1], t.k + 1)
                    ins = rows_by(bank[0:ROWS, :], 1, w2, r, slice(c * CHUNK, (c + 1) * CHUNK))
                elif name[0] == "v2":
                    _, r, c = name
                    n = VCHUNK + c * GATES_W
                    ins = rows_by(bank[0:ROWS, 0:n], 1, w2, r, slice(QK_W + c * VCHUNK, QK_W + c * VCHUNK + n))
                elif name[0] == "qk1":
                    h = name[1]
                    tt = terms(0, w1)
                    for k in range(2):
                        cols = slice(k * AH * AD + h * AD, k * AH * AD + (h + 1) * AD)
                        for i, (a, b) in enumerate(tt):
                            ins = nc.tensor.matmul(bank[0:AD, k * COLS:(k + 1) * COLS],
                                                   b[:, cols], a, start=(i == 0), stop=(i == len(tt) - 1))
                elif name[0] == "ft":
                    j = name[1]
                    for k in range(2):
                        for r in range(TILES):
                            if j == 0 and k == 0:
                                pe.wait_ge(s_qn, ev(t.k - 1, TILES, r))
                            a = k * V_W + j * 128
                            ins = nc.tensor.transpose(bank[:, k * COLS + r * ROWS:k * COLS + (r + 1) * ROWS],
                                                      qk2[:, r, a:a + 128], ident[0:ROWS, 0:ROWS])
                elif name[0] == "out":
                    r = name[1]
                    if r == 0:
                        pe.wait_ge(s_ctx, pair_ev(t, AG - 1))
                    for h in range(AH):
                        ins = nc.tensor.matmul(bank[0:ROWS, 0:DIM], ctx1[:, h, TILE_AT[r]], wo[:, h, :],
                                               start=(h == 0), stop=(h == AH - 1))
                else:
                    r = name[1]
                    if r == 0:
                        pe.wait_ge(s_ctx, pair_ev(t, -1))
                    for j in range(FG):
                        ins = nc.tensor.matmul(bank[0:ROWS, 0:DIM], ctx2[:, j, TILE_AT[r]], wp[:, j, :],
                                               start=(j == 0), stop=(j == FG - 1))
                q_filled(ins, name)

            def fill_or_pass(t, name):
                if t.has(name):
                    fill(t, name)
                else:
                    q_wait_free(pe, t, name)
                    pe.sem_inc(s_q_full[BANK_USE[name] % 2], 1)
                    pe.sem_inc(s_q_free[BANK_USE[name] % 2], 1)

            def score(t, g):
                if not t.head(g):
                    return pass_over(pe, s_score, head_ev(t, g))
                if AH > g - 2 >= 0 and t.att:
                    pe.wait_ge(s_logit, ev(t.k, AH, g - 2))
                else:
                    pe.wait_ge(s_exp, head_ev(t, g - 2))
                if g < AH:
                    pe.wait_ge(s_qkt, ev(t.k, AH, g))
                    q, k = qkt[g % 2][:, 0, :], qkt[g % 2][:, 1, :]
                else:
                    j = (g - AH) // 2
                    pe.wait_ge(s_fk, ev(t.k - 1, FG, j))
                    q, k = qz[j % 2][g % 2], kt[j % 2][:, :]
                for r in range(TILES):
                    ins = nc.tensor.matmul(bank_s[g % 2][0:ROWS, r * COLS:(r + 1) * COLS], q[:, TILE_AT[r]], k,
                                           start=True, stop=True)
                ins.then_inc(s_score, 1)

            def transpose_p(t, g):
                if t.head(g) is None:
                    return None
                if not t.head(g):
                    return pass_over(pe, s_pt, head_ev(t, g))
                pe.wait_ge(s_prob, head_ev(t, g))
                pe.wait_ge(s_pte[g % 2], pair_ev(t, g // 2 - 1))
                for kt_ in range(TILES):
                    for r in range(TILES):
                        ins = nc.tensor.transpose(
                            bank_t[g % 2][0:ROWS, kt_ * COLS + r * ROWS:kt_ * COLS + (r + 1) * ROWS],
                            prob[g % 4][:, r, TILE_AT[kt_]], ident[0:ROWS, 0:ROWS])
                ins.then_inc(s_pt, 1)

            def mix(t, g):
                if t.head(g) is None:
                    return None
                if not t.head(g):
                    return pass_over(pe, s_pv, head_ev(t, g))
                pe.wait_ge(s_pte[g % 2], pair_ev(t, g // 2))
                u = g // 2
                if g % 2 == 0:
                    pe.wait_ge(s_ctx, pair_ev(t, u - 2))
                bank = bank_c[u % 2]
                gg = g % HEADS
                if gg < AH:
                    o, v = bank[0:AD, (g % 2) * COLS:(g % 2 + 1) * COLS], v1
                    cols = slice(gg * AD, (gg + 1) * AD)
                    if gg == 0:
                        pe.wait_ge(s_v1, ev(t.k, 4, 3))
                else:
                    f = gg - AH
                    o, v = bank[(f % 2) * 64:(f % 2) * 64 + 64, 0:COLS], v2
                    cols = slice(f * FD, (f + 1) * FD)
                    if f == 0:
                        pe.wait_ge(s_v2, ev(t.k - 1, 4, 3))
                for kt_ in range(TILES):
                    n = KEYS[kt_]
                    ins = nc.tensor.matmul(o, v[0:n, kt_, cols], probt[g % 2][0:n, kt_, :],
                                           start=(kt_ == 0), stop=(kt_ == 1))
                ins.then_inc(s_pv, 1)

            def turn(t):
                for s in steps_of(t):
                    for name in FILL.get(s, []):
                        fill_or_pass(t, name)
                    transpose_p(t, s - LAG)
                    mix(t, s - LAG - 1)
                    if s in PREP:
                        fill_or_pass(t, PREP[s])
                    score(t, s)

            for s in (s_score, s_pt, s_pv):
                pe.sem_inc(s, 1)
            for t in turns_before():
                if t.k == 0:
                    pe.wait_ge(s_dist, 9 * 16)
                turn(t)
            with pe.Fori(0, LOOPS) as it:
                for p in range(2):
                    turn(loop_turn(it, p))
            for t in turns_after():
                turn(t)

        @block.scalar
        def _(act):
            def split_weights(tiles, first, n):
                for i, st in enumerate((stage_a, stage_c)):
                    act.wait_ge(s_staged, first + i + 1)
                    nc.scalar.activation(tiles[2 * i][:, :], st[:, 0:n], ACT.Copy).then_inc(s_whi, 1)

            act.wait_ge(s_wload, 32)
            for half in range(2):
                src = wtok_rows[:, half, :].rearrange("e (cr g w) -> e w g cr", g=2, w=PW)
                for w in range(PW):
                    ins = nc.scalar.activation(wtok_perm[:, half, w * 96:(w + 1) * 96]
                                               .rearrange("e (g cr) -> e g cr", g=2), src[:, w, :, :], ACT.Copy)
                ins.then_inc(s_wtok_p, 1)
            for n in range(16):
                act.wait_ge(s_wtok_t, n + 1)
                half, w = n // PW, n % PW
                nc.scalar.activation(wtok[:, w, half * 96:(half + 1) * 96], bank_t[n % 2][0:96, 0:96],
                                     ACT.Copy).then_inc(s_wtok_c, 1)
            split_weights(w1, 0, W1_W)

            split_weights(w2, 2, W2_W)

            def split_hi(t, name, n):
                q_full(act, t, name)
                nc.scalar.activation(xh[n][:, :, :].rearrange("p a n -> p (a n)"), q_bank(name)[:, 0:2 * COLS],
                                     ACT.Copy).then_inc(s_xhi[n], 1)

            def qk_copy(t, h):
                name = ("qk1", h)
                img = t.k + 1 if h == 0 else t.k
                q_full(act, t, name)
                act.wait_ge(s_score, head_ev(t, h - 2 if h >= 2 else AH - 1 if h == 0 else -1))
                nc.scalar.activation(qkt[h % 2][:, :, :].rearrange("p a n -> p (a n)"),
                                     q_bank(name)[0:AD, 0:2 * COLS], ACT.Copy).then_inc(s_qkt, 1)
                q_free(act, name, s_qkt, ev(img, AH, h))

            def turned(t, j):
                name = ("ft", j)
                q_full(act, t, name)
                act.wait_ge(s_score, head_ev(t, AH + 2 * (j - 2) + 1 if j >= 2 else -1))
                bank = q_bank(name)
                for a in range(2):
                    r = slice(64 * a, 64 * a + 64)
                    ins = nc.scalar.activation(qz[j % 2][a][r, :], bank[r, 0:COLS], ACT.Identity,
                                               bias=aff[r, 1:2], scale=aff[r, 0:1])
                ins.then_inc(s_ft, 1)

            def exps(t, g):
                if not t.head(g):
                    return pass_over(act, s_exp, head_ev(t, g))
                act.wait_ge(s_max, head_ev(t, g))
                act.wait_ge(s_pt, head_ev(t, g - 4))
                for r in range(TILES):
                    a = logits[g % 2][:, r, 0:SEQ] if g < AH else bank_s[g % 2][0:ROWS, r * COLS:r * COLS + SEQ]
                    ins = nc.scalar.activation(prob[g % 4][:, r, 0:SEQ], a, ACT.Exp,
                                               bias=negmax[g % 4][:, r:r + 1],
                                               accum_out=psumr[g % 4][:, r:r + 1])
                ins.then_inc(s_exp, 1)

            def pt_copy(t, g):
                if g % 2 or t.head(g) is None:
                    return None
                if not t.head(g):
                    return pass_over(act, s_pte[0], pair_ev(t, g // 2))
                act.wait_ge(s_pt, head_ev(t, g))
                act.wait_ge(s_pv, head_ev(t, g - 2))
                nc.scalar.activation(probt[0][:, :, :].rearrange("p a n -> p (a n)"),
                                     bank_t[0][0:ROWS, 0:2 * COLS], ACT.Copy).then_inc(s_pte[0], 1)

            def ctx_copy(t, u):
                if t.head(2 * u) is None:
                    return None
                if not t.head(2 * u):
                    return pass_over(act, s_ctx, pair_ev(t, u))
                act.wait_ge(s_pv, head_ev(t, 2 * u + 1))
                uu = u % (HEADS // 2)
                if uu < AG:
                    nc.scalar.activation(ctx1[:, 2 * uu:2 * uu + 2, :].rearrange("p a n -> p (a n)"),
                                         bank_c[u % 2][0:AD, 0:2 * COLS], ACT.Copy).then_inc(s_ctx, 1)
                else:
                    nc.scalar.activation(ctx2[:, uu - AG, :], bank_c[u % 2][:, 0:COLS],
                                         ACT.Copy).then_inc(s_ctx, 1)

            def squares(t, r):
                act.wait_ge(s_qk2, ev(t.k - 1, 6, r * 3 + 2))
                if r == 1:
                    act.wait_ge(s_ss, ev(t.k - 1, TILES, 0))
                nc.scalar.activation(sq[:, :], qk2[:, r, :], ACT.Square).then_inc(s_sq, 1)

            def turn(t):
                for s in steps_of(t):
                    if s % 2 == 0:
                        ctx_copy(t, (s - LAG - 3) // 2)
                    pt_copy(t, s - LAG)
                    if s in PREP and t.has(PREP[s]):
                        name = PREP[s]
                        if name[0] == "qk1":
                            qk_copy(t, name[1])
                        elif name[0] == "ft":
                            turned(t, name[1])
                        else:
                            split_hi(t, name, 0 if name[0] == "x1t" else 1)
                    exps(t, s)
                    if t.ffn and s in (1, 3):
                        squares(t, s // 2)
                    if t.ffn and s == 6:
                        act.wait_ge(s_glog, t.k)
                        nc.scalar.activation(gexp[:, :, 0:GATES_W], glog[:, :, 0:GATES_W],
                                             ACT.Exp).then_inc(s_gexp, 1)

            for s in (s_exp, s_pte[0], s_ctx):
                act.sem_inc(s, 1)
            for t in turns_before():
                turn(t)
            with act.Fori(0, LOOPS) as it:
                for p in range(2):
                    turn(loop_turn(it, p))
            for t in turns_after():
                turn(t)

        @block.vector
        def _(dve):
            chain = Steps(s_dve)

            def step(ins):
                chain.mark(ins)
                return ins

            def ready(apart=False):
                dve.wait_ge(s_dve, chain.value())
                if apart:
                    dve.sem_inc(s_apart, 1)

            dve.wait_ge(s_misc, 16 * N_MISC)
            r1 = 2 * MAX_DIST - 1 - 128
            step(nc.vector.reduce_sum(rel_sum[:, 0, :], rel_rows[:, 0, :, :], AX.X))
            step(nc.vector.reduce_sum(rel_sum[0:r1, 1, :], rel_rows[0:r1, 1, :, :], AX.X))
            step(nc.vector.tensor_tensor(posb[:, :, :], posb[:, :, :], h0[0][:, :, :], ALU.add))
            ready()
            step(nc.vector.tensor_copy(h0[0][:, :, :], posb[:, :, :]))
            step(nc.vector.tensor_copy(h0[1][:, :, :], posb[:, :, :]))
            step(nc.vector.tensor_scalar(aff[:, 0:2], aff[:, 0:2], float(FD) ** -0.5, None, ALU.mult))
            first = SEQ - 1 - (MAX_DIST - 1)
            dve.wait_ge(s_rel_t, 2)
            step(nc.vector.memset(ext[:, :], 0.0))
            ready()
            step(nc.vector.tensor_copy(ext[:, first:first + 128], bank_s[0][0:AH, 0:128]))
            step(nc.vector.tensor_copy(ext[:, first + 128:first + 128 + r1], bank_s[1][0:AH, 0:r1]))
            ready()
            step(nc.vector.tensor_scalar(ext[:, 0:first], ext[:, 0:first], ext[:, first:first + 1], None, ALU.add))
            e = first + 2 * MAX_DIST - 1
            step(nc.vector.tensor_scalar(ext[:, e:], ext[:, e:], ext[:, e - 1:e], None, ALU.add))
            ready()
            nc.vector.tensor_copy(ext[:, e:e + 1], ext[:, e + 1:e + 2]).then_inc(s_ext, 1)
            dve.wait_ge(s_stage1, 9 * 16)
            for st in (stage_a, stage_c):
                nc.vector.tensor_scalar(st[:, 0:AH * AD], st[:, 0:AH * AD], float(AD) ** -0.5, None,
                                        ALU.mult).then_inc(s_staged, 1)

            def split_weights(tiles, first, n):
                for i, st in enumerate((stage_a, stage_c)):
                    dve.wait_ge(s_whi, first + i + 1)
                    for half in range(2):
                        cols = slice(half * (n // 2), (half + 1) * (n // 2))
                        nc.vector.tensor_tensor(tiles[2 * i + 1][:, cols], st[:, cols],
                                                tiles[2 * i][:, cols].bitcast(F32), ALU.subtract).then_inc(s_wlo, 1)

            dve.wait_ge(s_staged, 2)
            split_weights(w1, 0, W1_W)

            dve.wait_ge(s_stage2, 12 * 16)
            for i, (st, rows) in enumerate(((stage_a, 128), (stage_c, 128), (bqk, ROWS))):
                view = st[0:rows, 0:QK_W].rearrange("p (h d) -> p h d", d=FD)
                step(nc.vector.reduce_sum(setup_mean[0:rows, :], view, AX.X))
                ready()
                step(nc.vector.tensor_scalar(setup_mean[0:rows, :], setup_mean[0:rows, :], 1.0 / FD, None, ALU.mult))
                ready()
                ins = nc.vector.tensor_tensor(view, view, setup_mean[0:rows, :].unsqueeze(2)
                                              .to_broadcast([rows, 2 * FH, FD]), ALU.subtract)
                if i < 2:
                    ins.then_inc(s_staged, 1)
                    dve.wait_ge(s_staged, 3 + i)
                else:
                    step(ins)
            split_weights(w2, 2, W2_W)
            step(nc.vector.memset(gexp[:, :, 4 + ROUTED:], -1.0))
            step(nc.vector.memset(gtop[:, :, :], -1.0))
            ready()
            dve.wait_ge(s_dist, 9 * 16)

            def statistics(h, n):
                for r in range(TILES):
                    step(nc.vector.bn_stats(bn[n][:, r, :], h[:, r, :]))
                ready(apart=True)
                for r in range(TILES):
                    step(nc.vector.bn_aggr(mv[n][:, r, :], bn[n][:, r, :]))
                ready()
                nc.vector.tensor_scalar(var[n][:, :], mv[n][:, :, 1], LN_EPS, None, ALU.add).then_inc(s_var[n], 1)

            def normalise(h, n, img):
                dve.wait_ge(s_rstd[n], img + 1)
                for r in range(TILES):
                    step(nc.vector.tensor_scalar(xn[n][:, r, 0:DIM], h[:, r, :], mv[n][:, r, 0:1],
                                                 rstd[n][:, r:r + 1], ALU.subtract, ALU.mult))
                ready()
                nc.vector.tensor_copy(xn[n][:, :, DIM:], xn[n][:, :, 128:DIM]).then_inc(s_xn[n], 1)

            def split_lo(t, name, n, img):
                dve.wait_ge(s_xhi[n], img + 1)
                bank = q_bank(name)
                step(nc.vector.tensor_tensor(xl[n][:, :], bank[:, 0:COLS], xh[n][:, 0, :].bitcast(F32), ALU.subtract))
                nc.vector.tensor_tensor(xh[n][64:128, 1, :], bank[64:128, COLS:2 * COLS],
                                        xh[n][64:128, 1, :].bitcast(F32), ALU.subtract).then_inc(s_xlo[n], 1)
                q_free(dve, name, s_xlo[n], img + 1)

            def by_tile(bank, rows, n):
                return bank[0:rows, 0:TILES * n].rearrange("p (t e) -> p t e", t=TILES)

            two = lambda a: a[:, :, 0:4].rearrange("p t (s n) -> p t s n", s=2)
            b2 = lambda a: a[:, :, 0:2].unsqueeze(3).to_broadcast([ROWS, TILES, 2, 2])
            b10 = lambda a: a.to_broadcast([ROWS, TILES, ROUTED])

            def add_bias(t, name):
                kind, r, c = name
                q_full(dve, t, name)
                if kind == "qk2":
                    img = t.k if name in EARLY else t.k - 1
                    cols, done, n = slice(c * CHUNK, (c + 1) * CHUNK), s_qk2, ev(img, 6, r * 3 + c)
                    nc.vector.tensor_tensor(qk2[:, r, cols], q_bank(name)[0:ROWS, :], bqk[:, cols],
                                            ALU.add).then_inc(s_qk2, 1)
                else:
                    cols, done, n = slice(c * VCHUNK, (c + 1) * VCHUNK), s_v2, ev(t.k - 1, 4, V2_ORDER.index((r, c)))
                    if (r, c) == V2_ORDER[0]:
                        dve.wait_ge(s_pv, head_ev(t, -1))
                    nc.vector.tensor_tensor(v2[:, r, cols], q_bank(name)[0:ROWS, 0:VCHUNK], bv[:, cols],
                                            ALU.add).then_inc(s_v2, 1)
                    if c == 1:
                        step(nc.vector.tensor_copy(glog[:, r, 0:GATES_W], q_bank(name)[0:ROWS, VCHUNK:VCHUNK + GATES_W]))
                        ready()
                q_free(dve, name, done, n)

            def v_copy(t, name):
                _, r, c = name
                q_full(dve, t, name)
                if (r, c) == (0, 0):
                    dve.wait_ge(s_pv, head_ev(t, AH - 1))
                nc.vector.tensor_copy(v1[:, r, c * VCHUNK:(c + 1) * VCHUNK],
                                      q_bank(name)[0:ROWS, 0:VCHUNK]).then_inc(s_v1, 1)
                q_free(dve, name, s_v1, ev(t.k + 1, 4, r * 2 + c))

            def turned_keys(t, j):
                name = ("ft", j)
                dve.wait_ge(s_ft, ev(t.k - 1, FG, j))
                dve.wait_ge(s_score, head_ev(t, AH + 2 * (j - 2) + 1 if j >= 2 else -1))
                nc.vector.tensor_scalar(kt[j % 2][:, :], q_bank(name)[:, COLS:2 * COLS], aff[:, 2:3], aff[:, 3:4],
                                        ALU.mult, ALU.add).then_inc(s_fk, 1)
                q_free(dve, name, s_fk, ev(t.k - 1, FG, j))

            def variance(t, r):
                dve.wait_ge(s_sq, ev(t.k - 1, TILES, r))
                nc.vector.reduce_sum(ss[:, r, :], sq[:, :].rearrange("p (h d) -> p h d", d=FD),
                                     AX.X).then_inc(s_ss, 1)
                dve.wait_ge(s_ss, ev(t.k - 1, TILES, r))
                nc.vector.tensor_scalar(ss[:, r, :], ss[:, r, :], 1.0 / FD, LN_EPS, ALU.mult,
                                        ALU.add).then_inc(s_qvar, 1)

            def normalise_qk(t, r):
                dve.wait_ge(s_qrstd, ev(t.k - 1, TILES, r))
                view = qk2[:, r, :].rearrange("p (h d) -> p h d", d=FD)
                nc.vector.tensor_tensor(view, view, ss[:, r, :].unsqueeze(2).to_broadcast([ROWS, 2 * FH, FD]),
                                        ALU.mult).then_inc(s_qn, 1)

            def gate_logits(t):
                lg = glog
                step(nc.vector.tensor_reduce(gmax[:, :, 0:2], two(lg), AX.X, ALU.max))
                step(nc.vector.tensor_reduce(gmax[:, :, 2:3], lg[:, :, 4:14], AX.X, ALU.max))
                ready()
                step(nc.vector.tensor_tensor(two(lg), two(lg), b2(gmax), ALU.subtract))
                ready()
                nc.vector.tensor_tensor(lg[:, :, 4:14], lg[:, :, 4:14], b10(gmax[:, :, 2:3]),
                                        ALU.subtract).then_inc(s_glog, 1)

            def gates_select(t):
                dve.wait_ge(s_gexp, t.k)
                ge = gexp
                step(nc.vector.tensor_reduce(gsum[:, :, 0:2], two(ge), AX.X, ALU.add))
                step(nc.vector.tensor_reduce(gsum[:, :, 2:3], ge[:, :, 4:14], AX.X, ALU.add))
                ready()
                step(nc.vector.reciprocal(gsum[:, :, :], gsum[:, :, :]))
                ready()
                step(nc.vector.tensor_tensor(two(glog), two(ge), b2(gsum), ALU.mult))
                step(nc.vector.tensor_tensor(ge[:, :, 4:14], ge[:, :, 4:14], b10(gsum[:, :, 2:3]), ALU.mult))
                ready(apart=True)
                for r in range(TILES):
                    step(nc.vector.max(gtop[:, r, :], ge[:, r, 4:14]))
                ready()
                step(nc.vector.memset(gtop[:, :, TOPK:], -1.0))
                ready(apart=True)
                for r in range(TILES):
                    step(nc.vector.match_replace(gcut[:, r, :], gtop[:, r, :], ge[:, r, 4:20], -2.0))
                ready()
                step(nc.vector.scalar_tensor_tensor(out=gsel[:, :, :], in0=gcut[:, :, 0:ROUTED], scalar=-1.5,
                                                    in1=ge[:, :, 4:14], op0=ALU.is_lt, op1=ALU.mult))

            def gates_scale(t):
                ready()
                step(nc.vector.tensor_reduce(gden[:, :], gsel[:, :, :], AX.X, ALU.add))
                ready()
                step(nc.vector.tensor_scalar(gden[:, :], gden[:, :], FLT_EPS, None, ALU.max))
                ready()
                step(nc.vector.reciprocal(gden[:, :], gden[:, :]))
                ready()
                step(nc.vector.scalar_tensor_tensor(out=gden[:, :], in0=gden[:, :], scalar=2.0 * TOPK,
                                                    in1=glog[:, :, 1], op0=ALU.mult, op1=ALU.mult))
                step(nc.vector.scalar_tensor_tensor(out=gate[:, :, 0:SHARED], in0=glog[:, :, 2:4],
                                                    scalar=2.0 * SHARED,
                                                    in1=glog[:, :, 0:1].to_broadcast([ROWS, TILES, SHARED]),
                                                    op0=ALU.mult, op1=ALU.mult))
                ready()
                step(nc.vector.tensor_tensor(gate[:, :, SHARED:], gsel[:, :, :],
                                             gden[:, :].unsqueeze(2).to_broadcast([ROWS, TILES, ROUTED]),
                                             ALU.mult))
                ready()

            def maxes(t, g):
                if not t.head(g):
                    return pass_over(dve, s_max, head_ev(t, g))
                dve.wait_ge(s_score, head_ev(t, g))
                bank = bank_s[g % 2]
                nm = negmax[g % 4]
                if g < AH:
                    dve.wait_ge(s_exp, head_ev(t, g - 2))
                    dve.sem_inc(s_apart, 1)
                    for r in range(TILES):
                        ins = nc.vector.tensor_tensor_reduce(
                            logits[g % 2][:, r, 0:SEQ], bank[0:ROWS, r * COLS:r * COLS + SEQ],
                            dist[:, r, g, 0:SEQ], 1.0, -3.0e38, ALU.add, ALU.max, nm[:, 2 + r:3 + r])
                    ins.then_inc(s_logit, 1)
                    dve.wait_ge(s_logit, ev(t.k, AH, g))
                    nc.vector.tensor_scalar(nm[:, 0:TILES], nm[:, 2:4], -1.0, None, ALU.mult).then_inc(s_max, 1)
                else:
                    dve.wait_ge(s_exp, head_ev(t, g - 4))
                    nc.vector.tensor_reduce(nm[:, 0:TILES], bank[0:ROWS, 0:2 * COLS]
                                            .rearrange("p (t k) -> p t k", t=TILES)[:, :, 0:SEQ],
                                            AX.X, ALU.max, negate=True).then_inc(s_max, 1)

            def recip(t, g):
                if t.head(g) is None:
                    return None
                if not t.head(g):
                    return pass_over(dve, s_rec, head_ev(t, g))
                dve.wait_ge(s_exp, head_ev(t, g))
                dve.wait_ge(s_prob, head_ev(t, g - 4))
                if g % HEADS < AH:
                    nc.vector.reciprocal(rec[g % 4][:, :], psumr[g % 4][:, :]).then_inc(s_rec, 1)
                else:
                    step(nc.vector.reciprocal(psumr[g % 4][:, :], psumr[g % 4][:, :]))
                    ready()
                    nc.vector.tensor_tensor(rec[g % 4][:, :], psumr[g % 4][:, :], gate[:, :, g % HEADS - AH],
                                            ALU.mult).then_inc(s_rec, 1)

            def pt_copy(t, g):
                if g % 2 == 0 or t.head(g) is None:
                    return None
                if not t.head(g):
                    return pass_over(dve, s_pte[1], pair_ev(t, g // 2))
                dve.wait_ge(s_pt, head_ev(t, g))
                dve.wait_ge(s_pv, head_ev(t, g - 2))
                nc.vector.tensor_copy(probt[1][:, :, :].rearrange("p a n -> p (a n)"),
                                      bank_t[1][0:ROWS, 0:2 * COLS]).then_inc(s_pte[1], 1)

            def new_h(t, r):
                q_full(dve, t, ("tok", r))
                step(nc.vector.tensor_tensor(h0[1 - t.p][0:HALF, r, :], q_bank(("tok", r))[0:HALF, 0:DIM],
                                             posb[0:HALF, r, :], ALU.add))
                q_free(dve, ("tok", r), s_dve, chain.value())
                if r == 1:
                    statistics(h0[1 - t.p], 0)

            def attended(t, r):
                q_full(dve, t, ("out", r))
                if r == 0 and not (isinstance(t.k, int) and t.k == 0):
                    dve.wait_ge(s_h1b, t.k)
                nc.vector.tensor_tensor(h1[:, r, :], q_bank(("out", r))[0:ROWS, 0:DIM], h0[t.p][:, r, :],
                                        ALU.add).then_inc(s_h1, 1)
                q_free(dve, ("out", r), s_h1, ev(t.k, TILES, r))
                if r == 1:
                    statistics(h1, 1)

            def output(t, r):
                q_full(dve, t, ("proj", r))
                if r == 0:
                    dve.wait_ge(s_out[t.p], (t.half - 1) * 48 + 16)
                    dve.wait_ge(s_h1b, t.k - 1)
                nc.vector.tensor_tensor(osb[t.p][:, r, :], q_bank(("proj", r))[0:ROWS, 0:DIM], h1b[t.p][:, r, :],
                                        ALU.add).then_inc(s_osb, 1)
                q_free(dve, ("proj", r), s_osb, ev(t.k - 2, TILES, r) + 1)

            def turn(t):
                for s in steps_of(t):
                    for name in FILL.get(s, []):
                        if name[0] in ("qk2", "v2") and t.has(name):
                            add_bias(t, name)
                        if name[0] == "proj" and t.proj:
                            output(t, name[1])
                        if name[0] == "tok" and t.tok:
                            new_h(t, name[1])
                        if name[0] == "out" and t.att:
                            attended(t, name[1])
                        if name[0] == "v1" and t.tok:
                            v_copy(t, name)
                    if s == 9 and t.tok:
                        normalise(h0[1 - t.p], 0, t.k + 1)
                    if s == 15 and t.att:
                        normalise(h1, 1, t.k)
                    pt_copy(t, s - LAG)
                    recip(t, s - 1)
                    if s in PREP and t.has(PREP[s]):
                        name = PREP[s]
                        if name[0] == "x1t":
                            split_lo(t, name, 0, t.k + 1)
                        if name[0] == "x2t":
                            split_lo(t, name, 1, t.k)
                    maxes(t, s)
                    if t.ffn:
                        if s in PREP and PREP[s][0] == "ft":
                            turned_keys(t, PREP[s][1])
                        if s in (2, 4):
                            variance(t, s // 2 - 1)
                        if s in (5, 6):
                            normalise_qk(t, s - 5)
                        if s == 5:
                            gate_logits(t)
                        if s == 7:
                            gates_select(t)
                        if s == 8:
                            gates_scale(t)

            for s in (s_max, s_rec, s_pte[1], s_osb):
                dve.sem_inc(s, 1)
            for t in turns_before():
                turn(t)
            base = chain.n
            with dve.Fori(0, LOOPS) as it:
                for p in range(2):
                    chain.base, chain.n = base + (it * 2 + p) * DVE_STEPS, 0
                    turn(loop_turn(it, p))
                    assert chain.n == DVE_STEPS, chain.n
            chain.base, chain.n = base + 2 * LOOPS * DVE_STEPS, 0
            for t in turns_after():
                turn(t)

        @block.gpsimd
        def _(pool):
            nc.gpsimd.memset(ident[:, :], 0.0).then_inc(s_ident, 1)
            nc.gpsimd.memset(eps_pow[:, :], -0.5).then_inc(s_ident, 1)
            pool.wait_ge(s_ident, 2)
            nc.gpsimd.affine_select(out=ident[:, :], in_=ident[:, :], compare_op=ALU.not_equal, fill=1.0,
                                    base=0, pattern=[[-1, 128]], channel_multiplier=1).then_inc(s_ident, 1)
            zeros = [posb[96:ROWS, 1, :], h0[0][96:ROWS, 1, :], dist[:, 1, :, :]]
            zeros += [qz[i][a][64 * (1 - a):64 * (2 - a), :] for i in range(2) for a in range(2)]
            zeros += [pr[:, :, SEQ:COLS] for pr in prob]
            for n, z in enumerate(zeros):
                pool.wait_ge(s_ident, 3 + n)
                nc.gpsimd.memset(z, 0.0).then_inc(s_ident, 1)
            pool.wait_ge(s_ident, N_ZEROED)

            def rsqrt(ready, value, done, a, b, n):
                pool.wait_ge(ready, value)
                nc.gpsimd.tensor_tensor(b, a, eps_pow[0:ROWS, 0:n], ALU.pow).then_inc(done, 1)

            def scale(t, g):
                if t.head(g) is None:
                    return None
                if not t.head(g):
                    return pass_over(pool, s_prob, head_ev(t, g))
                pool.wait_ge(s_rec, head_ev(t, g))
                pr = prob[g % 4][:, :, 0:SEQ]
                nc.gpsimd.tensor_tensor(pr, pr, rec[g % 4][:, :].unsqueeze(2).to_broadcast([ROWS, TILES, SEQ]),
                                        ALU.mult).then_inc(s_prob, 1)

            def turn(t):
                for s in steps_of(t):
                    if s == 8 and t.tok:
                        rsqrt(s_var[0], t.k + 2, s_rstd[0], var[0][:, :], rstd[0][:, :], TILES)
                    if s == 14 and t.att:
                        rsqrt(s_var[1], t.k + 1, s_rstd[1], var[1][:, :], rstd[1][:, :], TILES)
                    scale(t, s - 1)
                    if s in (2, 4) and t.ffn:
                        r = s // 2 - 1
                        rsqrt(s_qvar, ev(t.k - 1, TILES, r), s_qrstd, ss[:, r, :], ss[:, r, :], 2 * FH)
                    if s == 18 and t.att:
                        pool.wait_ge(s_h1, ev(t.k, TILES, 1))
                        if t.proj:
                            pool.wait_ge(s_osb, ev(t.k - 2, TILES, 1) + 1)
                        nc.gpsimd.tensor_tensor(h1b[t.p][:, :, :], h1[:, :, :],
                                                bproj[:, :].unsqueeze(1).to_broadcast([ROWS, TILES, DIM]),
                                                ALU.add).then_inc(s_h1b, 1)

            pool.sem_inc(s_prob, 1)
            for t in turns_before():
                turn(t)
            with pool.Fori(0, LOOPS) as it:
                for p in range(2):
                    turn(loop_turn(it, p))
            for t in turns_after():
                turn(t)


_INS = ["x", "L0_tok_W", "L0_tok_b", "L0_tok_class_token", "L0_tok_pos_embed", "L0_attn_w_q", "L0_attn_w_k",
        "L0_attn_w_v", "L0_attn_w_o", "L0_attn_rel_emb", "L0_ffn_qkv_w", "L0_ffn_qkv_b", "L0_ffn_q_norm_w",
        "L0_ffn_q_norm_b", "L0_ffn_k_norm_w", "L0_ffn_k_norm_b", "L0_ffn_wg_w", "L0_ffn_wg0_w", "L0_ffn_wg1_w",
        "L0_ffn_proj_w", "L0_ffn_proj_b"]
_OUTS = [((IMAGES, SEQ, DIM), "float32")]


def kernel(**inputs):
    import numpy as _np
    import concourse.bacc as _bacc
    from concourse import mybir as _mybir
    from concourse.bass_utils import run_bass_kernel_spmd as _run

    nc = _bacc.Bacc("TRN2", target_bir_lowering=False, num_devices=1)
    arrays, args = {}, []
    for name in _INS:
        a = _np.ascontiguousarray(inputs[name])
        arrays[f"in_{name}_dram"] = a
        args.append(nc.dram_tensor(f"in_{name}_dram", a.shape, _mybir.dt.from_np(a.dtype), kind="ExternalInput").ap())
    for i, (shape, dtype) in enumerate(_OUTS):
        dt = _mybir.dt.from_np(_np.dtype(dtype))
        args.append(nc.dram_tensor(f"out_{i}_dram", shape, dt, kind="ExternalOutput").ap())
    vit_kernel(nc, *args)
    r = _run(nc, [arrays], core_ids=[0])
    got = tuple(r.results[0][f"out_{i}_dram"] for i in range(len(_OUTS)))
    return got[0]
```

```python
from contextlib import ExitStack

import concourse.bass as bass
from concourse import mybir

ALU = mybir.AluOpType
ACT = mybir.ActivationFunctionType
AX = mybir.AxisListType
F32 = mybir.dt.float32
F32R = mybir.dt.float32r

IMAGES, CHANNELS, SIDE = 64, 3, 224
GRID = 14
PATCH = SIDE // GRID
DIM = 192
PATCHES = GRID * GRID
SEQ = PATCHES + 1
AH, AD = 8, 96
FH, FD = 12, 64
SHARED = 2
ROUTED = FH - SHARED
TOPK = 2
MAX_DIST = 100
LN_EPS = 1e-5
FLT_EPS = 1.1920929e-07

TILES = 2
HALF = PATCHES // TILES
ROWS = HALF + 1
COLS = TILES * ROWS
KEYS = (ROWS, HALF)
TILE_AT = (slice(0, ROWS), slice(ROWS, COLS))

PW = PATCH // 2
TOK_K = CHANNELS * PATCH
QK_W = 2 * FH * FD
V_W = FH * FD
GATES_W = 2 + SHARED + ROUTED
W1_W = 3 * AH * AD
W2_W = QK_W + V_W + GATES_W
CHUNK = 512
VCHUNK = 384
HEADS = AH + FH
AG, FG = AH // 2, FH // 2

LAG = 3
FILL = {
    0: [("qk2", 0, 1), ("qk2", 0, 2)], 1: [("qk2", 1, 0)], 2: [("qk2", 1, 1)], 3: [("qk2", 1, 2)],
    4: [("v2", 0, 1)], 5: [("v2", 1, 1)], 6: [("tok", 0)], 7: [("tok", 1)], 8: [("proj", 0)], 9: [("proj", 1)],
    10: [("v2", 0, 0)], 11: [("v2", 1, 0)], 13: [("out", 0)], 14: [("out", 1)],
    15: [("v1", 0, 0)], 16: [("v1", 0, 1)], 17: [("v1", 1, 0)], 18: [("v1", 1, 1)], 19: [("qk2", 0, 0)],
}
EARLY = [("qk2", 0, 0)]
PREP = {s: [("qk1", s + 1)] for s in range(AH - 1)}
PREP |= {7: [("ft", 0), ("ft", 1)], 12: [("x1t",)], 17: [("x2t",)], HEADS - 1: [("qk1", 0)]}
PREP |= {8: [("ft", 2)], 10: [("ft", 3)], 13: [("ft", 4)], 14: [("ft", 5)]}
BANK_ORDER = [u for s in range(HEADS) for u in FILL.get(s, []) + PREP.get(s, [])]
assert len(BANK_ORDER) % 2 == 0
BANK_USES = len(BANK_ORDER) // 2
BANK_USE = {name: n for n, name in enumerate(BANK_ORDER)}

V2_ORDER = [name[1:] for name in BANK_ORDER if name[0] == "v2"]

STACK_STEPS = {7: [0, 1]} | {AH - 2 + f: [f] for f in range(2, FH)}

TURNED_FIRST = [0, 3, 5]

DVE_STEPS = 50


class Turn:

    def __init__(self, k, parity, half, att, ffn, tok, proj, before):
        self.k, self.p, self.half = k, parity, half
        self.att, self.ffn, self.tok, self.proj = att, ffn, tok, proj
        self.before = before

    def has(self, name):
        if name[0] in ("tok", "x1t", "v1") or name == ("qk1", 0):
            return self.tok
        if name[0] in ("qk1", "out", "x2t") or name in EARLY:
            return self.att
        return self.proj if name[0] == "proj" else self.ffn

    def head(self, g):
        if g < 0:
            return self.before.head(g + HEADS) if self.before else None
        return self.att if g < AH else self.ffn


def turns_before():
    t = Turn(-1, 1, 0, False, False, True, False, None)
    yield t
    t = Turn(0, 0, 0, True, False, True, False, t)
    yield t
    yield Turn(1, 1, 0, True, True, True, False, t)


def loop_turn(it, p):
    full = Turn(None, None, None, True, True, True, True, None)
    return Turn(it * 2 + (2 + p), p, it + 1, True, True, True, True, full)


LOOPS = (IMAGES - 4) // 2


def turns_after():
    t = Turn(None, None, None, True, True, True, True, None)
    for k in range(2 + 2 * LOOPS, IMAGES + 2):
        t = Turn(k, k % 2, k // 2, k < IMAGES, k <= IMAGES, k < IMAGES - 1, True, t)
        yield t


LAST_STEP = 9


def steps_of(t):
    last = isinstance(t.k, int) and t.k == IMAGES + 1
    return range(LAST_STEP + 1 if last else HEADS)


class Steps:

    def __init__(self, sem, base=0):
        self.sem, self.base, self.n = sem, base, 0

    def mark(self, ins):
        ins.then_inc(self.sem, 1)
        self.n += 1

    def value(self):
        return self.base + self.n


def vit_kernel(nc, x, tok_w, tok_b, cls, pos, w_q, w_k, w_v, w_o, rel_emb, qkv_w, qkv_b,
               qn_w, qn_b, kn_w, kn_b, wg, wg0, wg1, proj_w, proj_b, out):
    ext_w = 2 * (SEQ - 1) + 1
    dist_dram = nc.dram_tensor("dist_ext", (AH, SEQ, ext_w), F32, kind="Internal").ap()
    with ExitStack() as ctx:
        def sb(name, shape, dt=F32):
            return ctx.enter_context(nc.sbuf_tensor(name, shape, dt))

        def ps(name, shape):
            return ctx.enter_context(nc.psum_tensor(name, shape, F32))

        def sem(name):
            return ctx.enter_context(nc.semaphore(name))

        ident = sb("ident", [128, 128])
        eps_pow = sb("eps_pow", [128, 2 * FH])
        w1 = [sb(f"w1_{n}", [128, W1_W], F32R) for n in ("hi_a", "lo_a", "hi_c", "lo_c")]
        w2 = [sb(f"w2_{n}", [128, W2_W], F32R) for n in ("hi_a", "lo_a", "hi_c", "lo_c")]
        wtok = sb("wtok", [2 * TOK_K, PW, DIM])
        wo = sb("wo", [AD, AH, DIM])
        wp = sb("wp", [128, FG, DIM])
        dist = sb("dist", [ROWS, TILES, AH, COLS])
        posb = sb("posb", [ROWS, TILES, DIM])
        bqk = sb("bqk", [ROWS, QK_W])
        bv = sb("bv", [ROWS, V_W])
        bproj = sb("bproj", [ROWS, DIM])
        aff = sb("aff", [128, 4])
        ximg = sb("ximg", [2 * TOK_K, GRID, SIDE])
        h0 = [sb(f"h0_{p}", [ROWS, TILES, DIM]) for p in range(2)]
        h1 = sb("h1", [ROWS, TILES, DIM])
        h1b = [sb(f"h1b{p}", [ROWS, TILES, DIM]) for p in range(2)]
        xn = sb("xn", [ROWS, TILES, DIM + 64])
        xh = [sb(f"xh{n}", [128, 2, COLS], F32R) for n in (1, 2)]
        xl = [sb(f"xl{n}", [128, COLS], F32R) for n in (1, 2)]
        values = sb("values", [128, 2, TILES * V_W])
        v1, v2 = (values[0:ROWS, n, :].rearrange("p (t e) -> p t e", t=TILES) for n in range(2))
        qkt = [sb(f"qkt{i}", [AD, 2, COLS]) for i in range(2)]
        prob = [sb(f"prob{i}", [ROWS, TILES, COLS]) for i in range(4)]
        negmax = [sb(f"negmax{i}", [ROWS, 2 * TILES]) for i in range(4)]
        psumr = [sb(f"rowsum{i}", [ROWS, TILES]) for i in range(4)]
        rec = [sb(f"rec{i}", [ROWS, TILES]) for i in range(4)]
        probt = [sb(f"probt{i}", [ROWS, TILES, COLS]) for i in range(2)]
        ctx1 = sb("ctx1", [AD, AH, COLS])
        ctx2 = sb("ctx2", [128, FG, COLS])
        qk2_full = sb("qk2", [128, TILES, QK_W])
        qk2 = qk2_full[0:ROWS, :, :]
        sq = sb("sq", [ROWS, QK_W // 2])
        ss = sb("ss", [ROWS, TILES, 2 * FH])
        turned_qk = [sb(f"turned_qk{i}", [128, 2, COLS]) for i in range(2)]
        stack = [[sb(f"stack{i}{a}", [128, 3, COLS], F32R) for a in range(2)] for i in range(2)]
        bn = [sb(f"bn{n}", [ROWS, TILES, 6]) for n in (1, 2)]
        mv = [sb(f"mv{n}", [ROWS, TILES, 2]) for n in (1, 2)]
        var = [sb(f"var{n}", [ROWS, TILES]) for n in (1, 2)]
        rstd = [sb(f"rstd{n}", [ROWS, TILES]) for n in (1, 2)]
        gmax = sb("gmax", [ROWS, TILES, 3])
        gsum = sb("gsum", [ROWS, TILES, 3])
        glog = sb("glog", [ROWS, TILES, 4 + 16])
        gexp = sb("gexp", [ROWS, TILES, 4 + 16])
        gtop = sb("gtop", [ROWS, TILES, 8])
        gcut = sb("gcut", [ROWS, TILES, 16])
        gsel = sb("gsel", [ROWS, TILES, ROUTED])
        gden = sb("gden", [ROWS, TILES])
        gate = sb("gate", [ROWS, TILES, FH])
        stage_a = qk2_full[:, :, :].rearrange("p t e -> p (t e)")
        stage_c = values[:, :, :].rearrange("p t e -> p (t e)")
        setup_mean = sb("setup_mean", [128, 2 * FH])
        wtok_scratch = ximg[:, :, :].rearrange("p a b -> p (a b)")[:, 0:4 * PATCH * TOK_K]
        wtok_scratch = wtok_scratch.rearrange("p (s n) -> p s n", s=4)
        wtok_rows, wtok_perm = wtok_scratch[:, 0:2, :], wtok_scratch[:, 2:4, :]
        rel_rows = [st[:, W1_W:W1_W + AH * AD].rearrange("p (h d) -> p h d", h=AH) for st in (stage_a, stage_c)]
        rel_sum = sb("rel_sum", [128, 2, AH])
        ext = probt[0][0:AH, :, :].rearrange("p t k -> p (t k)")[:, 0:ext_w]

        bank_s = [ps(f"bank_s{i}", [128, 512]) for i in range(2)]
        bank_t = [ps(f"bank_t{i}", [128, 512]) for i in range(2)]
        bank_c = [ps(f"bank_c{i}", [128, 512]) for i in range(2)]
        bank_q = [ps(f"bank_q{i}", [128, 512]) for i in range(2)]

        s_wload = sem("s_wload")
        s_stage1 = sem("s_stage1")
        s_stage2 = sem("s_stage2")
        s_misc = sem("s_misc")
        s_ident = sem("s_ident")
        s_staged = sem("s_staged")
        s_whi = sem("s_whi")
        s_wlo = sem("s_wlo")
        s_wtok_p = sem("s_wtok_p")
        s_wtok_t = sem("s_wtok_t")
        s_wtok_c = sem("s_wtok_c")
        s_rel_t = sem("s_rel_t")
        s_ext = sem("s_ext")
        s_ext_out = sem("s_ext_out")
        s_dist = sem("s_dist")
        s_dve = sem("s_dve")
        s_apart = sem("s_apart")
        s_x = sem("s_x")
        s_q_full = [sem(f"s_q_full{i}") for i in range(2)]
        s_q_free = [sem(f"s_q_free{i}") for i in range(2)]
        s_var, s_rstd, s_xn, s_xhi, s_xlo = (
            [sem(f"s_{what}{n}") for n in (1, 2)] for what in ("var", "rstd", "xn", "xhi", "xlo"))
        s_qvar = sem("s_qvar")
        s_v1 = [sem("s_v1_dve"), sem("s_v1_act")]
        s_qkt = sem("s_qkt")
        s_score = sem("s_score")
        s_logit = sem("s_logit")
        s_max = sem("s_max")
        s_exp = sem("s_exp")
        s_rec = sem("s_rec")
        s_prob = sem("s_prob")
        s_pt = sem("s_pt")
        s_pte = [sem(f"s_pte{i}") for i in range(2)]
        s_pv = sem("s_pv")
        s_ctx = sem("s_ctx")
        s_h1 = sem("s_h1")
        s_h1b = sem("s_h1b")
        s_qk2 = sem("s_qk2")
        s_sq = sem("s_sq")
        s_ss = sem("s_ss")
        s_qrstd = sem("s_qrstd")
        s_qn = sem("s_qn")
        s_v2 = sem("s_v2")
        s_glog = sem("s_glog")
        s_gexp = sem("s_gexp")
        s_ft = sem("s_ft")
        s_high = sem("s_high")
        s_lowq = sem("s_lowq")
        s_low = sem("s_low")
        s_osb = sem("s_osb")
        s_out = [sem(f"s_out{p}") for p in range(2)]

        def ev(img, per_image, n):
            return img * per_image + n + 1

        def head_ev(t, g):
            return (t.k + 1) * HEADS + (g + 2)

        def pair_ev(t, u):
            return (t.k + 1) * (HEADS // 2) + (u + 2)

        def pass_over(eng, sem_, value):
            eng.wait_ge(sem_, value - 1)
            eng.sem_inc(sem_, 1)

        def rows_of_pair(a):
            return slice(64 * a, 64 * a + 64), slice(64 * (1 - a), 64 * (2 - a))

        def q_bank(name):
            return bank_q[BANK_USE[name] % 2]

        def q_full(eng, t, name):
            n = BANK_USE[name]
            eng.wait_ge(s_q_full[n % 2], (t.k + 1) * BANK_USES + (n // 2 + 1))

        def q_wait_free(eng, t, name):
            n = BANK_USE[name]
            value = (t.k + 1) * BANK_USES + n // 2
            if not isinstance(value, int) or value > 0:
                eng.wait_ge(s_q_free[n % 2], value)

        def q_filled(ins, name):
            ins.then_inc(s_q_full[BANK_USE[name] % 2], 1)

        def q_free(eng, name, done, value):
            eng.wait_ge(done, value)
            eng.sem_inc(s_q_free[BANK_USE[name] % 2], 1)

        block = ctx.enter_context(nc.Block())

        x_rows = x.rearrange("n c (i r) w -> n c r i w", r=PATCH)
        N_MISC = 4 + 2 + 2 + 1 + 8 + 2 + AH + FG
        N_ZEROED = 3 + 7 + 4

        @block.sync
        def _(sp):
            def load_w1(dst_rows, src_rows):
                n = src_rows.stop - src_rows.start
                for k, w in enumerate((w_q, w_k, w_v)):
                    for dst, at in dst_rows:
                        o = dst[at:at + n, k * AH * AD:(k + 1) * AH * AD].rearrange("e (h d) -> e h d", h=AH)
                        sp.dma_start(o, w[:, src_rows, :].rearrange("h e d -> e h d")).then_inc(s_stage1, 16)

            for half in range(2):
                sp.dma_start(wtok_rows[:, half, :], tok_w[half * 96:(half + 1) * 96, :]).then_inc(s_wload, 16)
            load_w1([(stage_a, 0)], slice(0, 128))
            load_w1([(stage_c, 0), (stage_c, 64)], slice(128, DIM))
            row = lambda a: a.rearrange("(o n) -> o n", o=1)
            sp.wait_ge(s_ident, N_ZEROED)
            for t in range(TILES):
                sp.dma_start(posb[0:HALF, t, :], pos[1 + t * HALF:1 + (t + 1) * HALF, :]).then_inc(s_misc, 16)
                sp.dma_start(h0[0][0:HALF, t, :], row(tok_b).to_broadcast([HALF, DIM])).then_inc(s_misc, 16)
            sp.dma_start(posb[HALF:ROWS, 0, :], pos[0:1, :]).then_inc(s_misc, 16)
            sp.dma_start(h0[0][HALF:ROWS, 0, :], cls).then_inc(s_misc, 16)
            sp.dma_start(bqk[:, :], row(qkv_b[0:QK_W]).to_broadcast([ROWS, QK_W])).then_inc(s_misc, 16)
            sp.dma_start(bv[:, :], row(qkv_b[QK_W:QK_W + V_W]).to_broadcast([ROWS, V_W])).then_inc(s_misc, 16)
            sp.dma_start(bproj[:, :], row(proj_b).to_broadcast([ROWS, DIM])).then_inc(s_misc, 16)
            for n, v in enumerate((qn_w, qn_b, kn_w, kn_b)):
                for half in range(2):
                    sp.dma_start(aff[half * 64:half * 64 + 64, n:n + 1],
                                 v.rearrange("(d o) -> d o", o=1)).then_inc(s_misc, 16)
            sp.dma_start(rel_rows[0],
                         rel_emb[:, 0:128, :, 0].rearrange("h r d -> r h d")).then_inc(s_misc, 16)
            sp.dma_start(rel_rows[1][0:2 * MAX_DIST - 1 - 128, :, :],
                         rel_emb[:, 128:2 * MAX_DIST - 1, :, 0].rearrange("h r d -> r h d")).then_inc(s_misc, 16)
            for h in range(AH):
                sp.dma_start(wo[:, h, :], w_o[h, :, :]).then_inc(s_misc, 16)
            for g in range(FG):
                sp.dma_start(wp[:, g, :], proj_w[g * 128:(g + 1) * 128, :]).then_inc(s_misc, 16)
            def load_x(img):
                for g in range(2):
                    for c in range(CHANNELS):
                        part = slice(g * TOK_K + c * PATCH, g * TOK_K + (c + 1) * PATCH)
                        w = SIDE - g * PW
                        src = x_rows[img, c, :, :, g * PW:SIDE] if isinstance(img, int) else \
                            x_rows[bass.ds(img, 1), c, :, :, g * PW:SIDE].rearrange("n r i w -> (n r) i w")
                        sp.dma_start(ximg[part, :, 0:w], src).then_inc(s_x, 16)

            sp.wait_ge(s_wtok_t, 16)
            load_x(0)
            sp.wait_ge(s_wlo, 4)
            for dst, at, a, b in ((stage_a, 0, 0, 128), (stage_c, 0, 128, DIM), (stage_c, 64, 128, DIM)):
                rows = slice(at, at + b - a)
                sp.dma_start(dst[rows, 0:QK_W + V_W], qkv_w[a:b, :]).then_inc(s_stage2, 16)
                g = QK_W + V_W
                sp.dma_start(dst[rows, g:g + 2], wg0[a:b, :]).then_inc(s_stage2, 16)
                sp.dma_start(dst[rows, g + 2:g + 4], wg1[a:b, :]).then_inc(s_stage2, 16)
                sp.dma_start(dst[rows, g + 4:g + 14], wg[a:b, :]).then_inc(s_stage2, 16)
            sp.wait_ge(s_ext, 1)
            sp.dma_start(dist_dram, ext[:, :].unsqueeze(1).to_broadcast([AH, SEQ, ext_w])).then_inc(s_ext_out, 16)
            sp.wait_ge(s_ext_out, 16)
            for rows, t, q0, nq in ((slice(0, HALF), 0, 1, HALF), (slice(HALF, ROWS), 0, 0, 1),
                                    (slice(0, HALF), 1, 1 + HALF, HALF)):
                for at, k0, nk in ((0, 1, HALF), (HALF, 0, 1), (ROWS, 1 + HALF, HALF)):
                    src = bass.AP(dist_dram.tensor, q0 * (ext_w - 1) + k0 + SEQ - 1,
                                 [[ext_w - 1, nq], [SEQ * ext_w, AH], [1, nk]])
                    sp.dma_start(dist[rows, t, :, at:at + nk], src, allow_slow_non_contiguous=nk == 1).then_inc(s_dist, 16)

            for p in range(2):
                sp.sem_inc(s_out[p], 16)

            def turn(t):
                if t.proj:
                    img = t.k - 2
                    sp.wait_ge(s_osb, ev(img, TILES, 1) + 1)
                    at = (lambda a, b: out[img, a:b, :]) if isinstance(img, int) else \
                        (lambda a, b: out[bass.ds(img, 1), a:b, :].rearrange("n s e -> (n s) e"))
                    o = h1b[t.p]
                    sp.dma_start(at(1, ROWS), o[0:HALF, 0, :]).then_inc(s_out[t.p], 16)
                    sp.dma_start(at(0, 1), o[HALF:ROWS, 0, :]).then_inc(s_out[t.p], 16)
                    sp.dma_start(at(ROWS, SEQ), o[0:HALF, 1, :]).then_inc(s_out[t.p], 16)
                if t.tok and not (isinstance(t.k, int) and t.k + 2 >= IMAGES):
                    q_full(sp, t, ("tok", 1))
                    load_x(t.k + 2)

            for t in turns_before():
                turn(t)
            with sp.Fori(0, LOOPS) as it:
                for p in range(2):
                    turn(loop_turn(it, p))
            for t in turns_after():
                turn(t)
            for p in range(2):
                sp.wait_ge(s_out[p], 48 * (IMAGES // 2) + 16)

        @block.tensor
        def _(pe):
            pe.wait_ge(s_ident, N_ZEROED)
            pe.wait_ge(s_wtok_p, 2)
            for half in range(2):
                rows = wtok_perm[:, half, :].rearrange("e (w k) -> e w k", w=PW)
                for w in range(PW):
                    n = half * PW + w
                    if n >= 2:
                        pe.wait_ge(s_wtok_c, n - 1)
                    nc.tensor.transpose(bank_t[n % 2][0:96, 0:96], rows[:, w, :],
                                        ident[0:96, 0:96]).then_inc(s_wtok_t, 1)
            pe.wait_ge(s_dve, 2)
            r1 = 2 * MAX_DIST - 1 - 128
            nc.tensor.transpose(bank_s[0][0:AH, 0:128], rel_sum[:, 0, :], ident[:, :]).then_inc(s_rel_t, 1)
            nc.tensor.transpose(bank_s[1][0:AH, 0:r1], rel_sum[0:r1, 1, :], ident[0:r1, 0:r1]).then_inc(s_rel_t, 1)

            def embed(bank, r):
                for w in range(PW):
                    cols = ximg[:, r * 7:(r + 1) * 7, :].rearrange("k i (j w) -> k i j w", w=PATCH)[:, :, :, w]
                    ins = nc.tensor.matmul(bank[0:HALF, 0:DIM], cols, wtok[:, w, :],
                                           start=(w == 0), stop=(w == PW - 1))
                return ins

            def transpose_x(bank, n):
                for t in range(TILES):
                    nc.tensor.transpose(bank[:, t * ROWS:(t + 1) * ROWS], xn[:, t, 0:128], ident[0:ROWS, 0:ROWS])
                    ins = nc.tensor.transpose(bank[:, COLS + t * ROWS:COLS + (t + 1) * ROWS],
                                              xn[:, t, 128:256], ident[0:ROWS, 0:ROWS])
                return ins

            def terms(n, w):
                hi_a, lo_a, hi_c, lo_c = w
                return [(xh[n][:, 0, :], lo_a), (xl[n][:, :], hi_a), (xh[n][:, 1, :], lo_c),
                        (xh[n][:, 1, :], hi_c), (xh[n][:, 0, :], hi_a)]

            def rows_by(bank_out, n, w, t, cols):
                tt = terms(n, w)
                for i, (a, b) in enumerate(tt):
                    ins = nc.tensor.matmul(bank_out, a[:, TILE_AT[t]], b[:, cols], start=(i == 0), stop=(i == len(tt) - 1))
                return ins

            pe.wait_ge(s_wtok_c, 16)

            def fill(t, name):
                q_wait_free(pe, t, name)
                bank = q_bank(name)
                if name[0] == "tok":
                    if name[1] == 0:
                        pe.wait_ge(s_x, (t.k + 2) * (2 * CHANNELS * 16))
                    ins = embed(bank, name[1])
                elif name[0] == "x1t":
                    pe.wait_ge(s_xn[0], t.k + 2)
                    ins = transpose_x(bank, 0)
                elif name[0] == "x2t":
                    pe.wait_ge(s_xn[1], t.k + 1)
                    ins = transpose_x(bank, 1)
                elif name[0] == "v1":
                    _, r, c = name
                    if (r, c) == (0, 0):
                        pe.wait_ge(s_xlo[0], t.k + 2)
                    ins = rows_by(bank[0:ROWS, 0:VCHUNK], 0, w1, r,
                                  slice(2 * AH * AD + c * VCHUNK, 2 * AH * AD + (c + 1) * VCHUNK))
                elif name[0] == "qk2":
                    _, r, c = name
                    if (r, c) == (0, 0):
                        pe.wait_ge(s_xlo[1], t.k + 1)
                    ins = rows_by(bank[0:ROWS, :], 1, w2, r, slice(c * CHUNK, (c + 1) * CHUNK))
                elif name[0] == "v2":
                    _, r, c = name
                    n = VCHUNK + c * GATES_W
                    ins = rows_by(bank[0:ROWS, 0:n], 1, w2, r, slice(QK_W + c * VCHUNK, QK_W + c * VCHUNK + n))
                elif name[0] == "qk1":
                    h = name[1]
                    tt = terms(0, w1)
                    for k in range(2):
                        cols = slice(k * AH * AD + h * AD, k * AH * AD + (h + 1) * AD)
                        for i, (a, b) in enumerate(tt):
                            ins = nc.tensor.matmul(bank[0:AD, k * COLS:(k + 1) * COLS],
                                                   b[:, cols], a, start=(i == 0), stop=(i == len(tt) - 1))
                elif name[0] == "ft":
                    j = name[1]
                    for k in range(2):
                        for r in range(TILES):
                            if j == 0 and k == 0:
                                pe.wait_ge(s_qn, ev(t.k - 1, TILES, r))
                            a = k * V_W + j * 128
                            ins = nc.tensor.transpose(bank[:, k * COLS + r * ROWS:k * COLS + (r + 1) * ROWS],
                                                      qk2[:, r, a:a + 128], ident[0:ROWS, 0:ROWS])
                elif name[0] == "out":
                    r = name[1]
                    if r == 0:
                        pe.wait_ge(s_ctx, pair_ev(t, AG - 1))
                    for h in range(AH):
                        ins = nc.tensor.matmul(bank[0:ROWS, 0:DIM], ctx1[:, h, TILE_AT[r]], wo[:, h, :],
                                               start=(h == 0), stop=(h == AH - 1))
                else:
                    r = name[1]
                    if r == 0:
                        pe.wait_ge(s_ctx, pair_ev(t, -1))
                    for j in range(FG):
                        ins = nc.tensor.matmul(bank[0:ROWS, 0:DIM], ctx2[:, j, TILE_AT[r]], wp[:, j, :],
                                               start=(j == 0), stop=(j == FG - 1))
                q_filled(ins, name)

            def fill_or_pass(t, name):
                if t.has(name):
                    fill(t, name)
                else:
                    q_wait_free(pe, t, name)
                    pe.sem_inc(s_q_full[BANK_USE[name] % 2], 1)
                    pe.sem_inc(s_q_free[BANK_USE[name] % 2], 1)

            def score(t, g):
                if not t.head(g):
                    return pass_over(pe, s_score, head_ev(t, g))
                if AH > g - 2 >= 0 and t.att:
                    pe.wait_ge(s_logit, ev(t.k, AH, g - 2))
                else:
                    pe.wait_ge(s_exp, head_ev(t, g - 2))
                if g < AH:
                    pe.wait_ge(s_qkt, ev(t.k, AH, g))
                    q, k = qkt[g % 2][:, 0, :], qkt[g % 2][:, 1, :]
                else:
                    j = (g - AH) // 2
                    pe.wait_ge(s_high, ev(t.k - 1, FH, g - AH))
                    pe.wait_ge(s_low, ev(t.k - 1, FH, g - AH))
                    st = stack[j % 2][g % 2]
                for r in range(TILES):
                    o = bank_s[g % 2][0:ROWS, r * COLS:(r + 1) * COLS]
                    if g < AH:
                        ins = nc.tensor.matmul(o, q[:, TILE_AT[r]], k, start=True, stop=True)
                    else:
                        nc.tensor.matmul(o, st[:, 0, TILE_AT[r]], st[:, 1, :], start=True, stop=False)
                        ins = nc.tensor.matmul(o, st[:, 0, TILE_AT[r]], st[:, 2, :], start=False, stop=True)
                ins.then_inc(s_score, 1)

            def transpose_p(t, g):
                if t.head(g) is None:
                    return None
                if not t.head(g):
                    return pass_over(pe, s_pt, head_ev(t, g))
                pe.wait_ge(s_prob, head_ev(t, g))
                pe.wait_ge(s_pte[g % 2], pair_ev(t, g // 2 - 1))
                for kt_ in range(TILES):
                    for r in range(TILES):
                        ins = nc.tensor.transpose(
                            bank_t[g % 2][0:ROWS, kt_ * COLS + r * ROWS:kt_ * COLS + (r + 1) * ROWS],
                            prob[g % 4][:, r, TILE_AT[kt_]], ident[0:ROWS, 0:ROWS])
                ins.then_inc(s_pt, 1)

            def mix(t, g):
                if t.head(g) is None:
                    return None
                if not t.head(g):
                    return pass_over(pe, s_pv, head_ev(t, g))
                pe.wait_ge(s_pte[g % 2], pair_ev(t, g // 2))
                u = g // 2
                if g % 2 == 0:
                    pe.wait_ge(s_ctx, pair_ev(t, u - 2))
                bank = bank_c[u % 2]
                gg = g % HEADS
                if gg < AH:
                    o, v = bank[0:AD, (g % 2) * COLS:(g % 2 + 1) * COLS], v1
                    cols = slice(gg * AD, (gg + 1) * AD)
                    if gg == 0:
                        for part in s_v1:
                            pe.wait_ge(part, ev(t.k, TILES, 1))
                else:
                    f = gg - AH
                    o, v = bank[(f % 2) * 64:(f % 2) * 64 + 64, 0:COLS], v2
                    cols = slice(f * FD, (f + 1) * FD)
                    if f == 0:
                        pe.wait_ge(s_v2, ev(t.k - 1, 4, 3))
                for kt_ in range(TILES):
                    n = KEYS[kt_]
                    ins = nc.tensor.matmul(o, v[0:n, kt_, cols], probt[g % 2][0:n, kt_, :],
                                           start=(kt_ == 0), stop=(kt_ == 1))
                ins.then_inc(s_pv, 1)

            def turn(t):
                for s in steps_of(t):
                    for name in FILL.get(s, []):
                        fill_or_pass(t, name)
                    transpose_p(t, s - LAG)
                    mix(t, s - LAG - 1)
                    for name in PREP.get(s, []):
                        fill_or_pass(t, name)
                    score(t, s)

            for s in (s_score, s_pt, s_pv):
                pe.sem_inc(s, 1)
            for t in turns_before():
                if t.k == 0:
                    pe.wait_ge(s_dist, 9 * 16)
                turn(t)
            with pe.Fori(0, LOOPS) as it:
                for p in range(2):
                    turn(loop_turn(it, p))
            for t in turns_after():
                turn(t)

        @block.scalar
        def _(act):
            def split_weights(tiles, first, n):
                for i, st in enumerate((stage_a, stage_c)):
                    act.wait_ge(s_staged, first + i + 1)
                    nc.scalar.activation(tiles[2 * i][:, :], st[:, 0:n], ACT.Copy).then_inc(s_whi, 1)

            act.wait_ge(s_wload, 32)
            for half in range(2):
                src = wtok_rows[:, half, :].rearrange("e (cr g w) -> e w g cr", g=2, w=PW)
                for w in range(PW):
                    ins = nc.scalar.activation(wtok_perm[:, half, w * 96:(w + 1) * 96]
                                               .rearrange("e (g cr) -> e g cr", g=2), src[:, w, :, :], ACT.Copy)
                ins.then_inc(s_wtok_p, 1)
            for n in range(16):
                act.wait_ge(s_wtok_t, n + 1)
                half, w = n // PW, n % PW
                nc.scalar.activation(wtok[:, w, half * 96:(half + 1) * 96], bank_t[n % 2][0:96, 0:96],
                                     ACT.Copy).then_inc(s_wtok_c, 1)
            split_weights(w1, 0, W1_W)

            split_weights(w2, 2, W2_W)

            def split_hi(t, name, n):
                q_full(act, t, name)
                nc.scalar.activation(xh[n][:, :, :].rearrange("p a n -> p (a n)"), q_bank(name)[:, 0:2 * COLS],
                                     ACT.Copy).then_inc(s_xhi[n], 1)

            def v_copy(t, r):
                name = ("v1", r, 1)
                q_full(act, t, name)
                act.wait_ge(s_pv, head_ev(t, AH - 1))
                nc.scalar.activation(v1[:, r, VCHUNK:], q_bank(name)[0:ROWS, 0:VCHUNK],
                                     ACT.Copy).then_inc(s_v1[1], 1)
                q_free(act, name, s_v1[1], ev(t.k + 1, TILES, r))

            def qk_copy(t, h):
                name = ("qk1", h)
                img = t.k + 1 if h == 0 else t.k
                q_full(act, t, name)
                act.wait_ge(s_score, head_ev(t, h - 2 if h >= 2 else AH - 1 if h == 0 else -1))
                nc.scalar.activation(qkt[h % 2][:, :, :].rearrange("p a n -> p (a n)"),
                                     q_bank(name)[0:AD, 0:2 * COLS], ACT.Copy).then_inc(s_qkt, 1)
                q_free(act, name, s_qkt, ev(img, AH, h))

            def turned(t, j):
                name = ("ft", j)
                q_full(act, t, name)
                if j >= 2:
                    act.wait_ge(s_low, ev(t.k - 1, FH, 2 * (j - 2) + 1))
                else:
                    act.wait_ge(s_score, head_ev(t, 2 * (j - 2) + 1))
                bank = q_bank(name)
                for n in range(2):
                    nc.scalar.activation(turned_qk[j % 2][:, n, :], bank[:, n * COLS:(n + 1) * COLS], ACT.Identity,
                                         bias=aff[:, 2 * n + 1:2 * n + 2],
                                         scale=aff[:, 2 * n:2 * n + 1]).then_inc(s_ft, 1)
                q_free(act, name, s_ft, ev(t.k - 1, FH, 2 * j + 1))

            def exps(t, g):
                if not t.head(g):
                    return pass_over(act, s_exp, head_ev(t, g))
                act.wait_ge(s_max, head_ev(t, g))
                if g >= AH:
                    act.wait_ge(s_pt, head_ev(t, g - 4))
                for r in range(TILES):
                    a = prob[g % 4][:, r, 0:SEQ] if g < AH else bank_s[g % 2][0:ROWS, r * COLS:r * COLS + SEQ]
                    ins = nc.scalar.activation(prob[g % 4][:, r, 0:SEQ], a, ACT.Exp,
                                               bias=negmax[g % 4][:, r:r + 1],
                                               accum_out=psumr[g % 4][:, r:r + 1])
                ins.then_inc(s_exp, 1)

            def pt_copy(t, g):
                if t.head(g) is None:
                    return None
                if not t.head(g):
                    return pass_over(act, s_pte[g % 2], pair_ev(t, g // 2))
                act.wait_ge(s_pt, head_ev(t, g))
                act.wait_ge(s_pv, head_ev(t, g - 2))
                nc.scalar.activation(probt[g % 2][:, :, :].rearrange("p a n -> p (a n)"),
                                     bank_t[g % 2][0:ROWS, 0:2 * COLS], ACT.Copy).then_inc(s_pte[g % 2], 1)

            def ctx_copy(t, u):
                if t.head(2 * u) is None:
                    return None
                if not t.head(2 * u):
                    return pass_over(act, s_ctx, pair_ev(t, u))
                act.wait_ge(s_pv, head_ev(t, 2 * u + 1))
                uu = u % (HEADS // 2)
                if uu < AG:
                    nc.scalar.activation(ctx1[:, 2 * uu:2 * uu + 2, :].rearrange("p a n -> p (a n)"),
                                         bank_c[u % 2][0:AD, 0:2 * COLS], ACT.Copy).then_inc(s_ctx, 1)
                else:
                    nc.scalar.activation(ctx2[:, uu - AG, :], bank_c[u % 2][:, 0:COLS],
                                         ACT.Copy).then_inc(s_ctx, 1)

            def squares(t, n):
                r, half = n // 2, n % 2
                act.wait_ge(s_qk2, ev(t.k - 1, 6, r * 3 + half + 1))
                if n > 0:
                    act.wait_ge(s_ss, ev(t.k - 1, 4, n - 1))
                nc.scalar.activation(sq[:, :], qk2[:, r, half * V_W:(half + 1) * V_W], ACT.Square).then_inc(s_sq, 1)

            def turn(t):
                for s in steps_of(t):
                    for name in FILL.get(s, []):
                        if name[0] == "v1" and name[2] == 1 and t.tok:
                            v_copy(t, name[1])
                    pt_copy(t, s - LAG)
                    for name in PREP.get(s, []):
                        if not t.has(name):
                            continue
                        if name[0] == "qk1":
                            qk_copy(t, name[1])
                        elif name[0] == "ft" and name[1] in TURNED_FIRST:
                            turned(t, name[1])
                        elif name[0] != "ft":
                            split_hi(t, name, 0 if name[0] == "x1t" else 1)
                    exps(t, s)
                    if s % 2:
                        ctx_copy(t, (s - LAG - 2) // 2)
                    for name in PREP.get(s, []):
                        if name[0] == "ft" and name[1] not in TURNED_FIRST and t.ffn:
                            turned(t, name[1])
                    if t.ffn and s < 4:
                        squares(t, s)
                    if t.ffn and s == 6:
                        act.wait_ge(s_glog, t.k)
                        nc.scalar.activation(gexp[:, :, 0:GATES_W], glog[:, :, 0:GATES_W],
                                             ACT.Exp).then_inc(s_gexp, 1)

            for s in (s_exp, *s_pte, s_ctx):
                act.sem_inc(s, 1)
            for t in turns_before():
                turn(t)
            with act.Fori(0, LOOPS) as it:
                for p in range(2):
                    turn(loop_turn(it, p))
            for t in turns_after():
                turn(t)

        @block.vector
        def _(dve):
            chain = Steps(s_dve)

            def step(ins):
                chain.mark(ins)
                return ins

            def ready(apart=False):
                dve.wait_ge(s_dve, chain.value())
                if apart:
                    dve.sem_inc(s_apart, 1)

            dve.wait_ge(s_misc, 16 * N_MISC)
            r1 = 2 * MAX_DIST - 1 - 128
            step(nc.vector.reduce_sum(rel_sum[:, 0, :], rel_rows[0], AX.X))
            step(nc.vector.reduce_sum(rel_sum[0:r1, 1, :], rel_rows[1][0:r1, :, :], AX.X))
            step(nc.vector.tensor_tensor(posb[:, :, :], posb[:, :, :], h0[0][:, :, :], ALU.add))
            ready()
            step(nc.vector.tensor_copy(h0[0][:, :, :], posb[:, :, :]))
            step(nc.vector.tensor_copy(h0[1][:, :, :], posb[:, :, :]))
            step(nc.vector.tensor_scalar(aff[:, 0:2], aff[:, 0:2], float(FD) ** -0.5, None, ALU.mult))
            first = SEQ - 1 - (MAX_DIST - 1)
            dve.wait_ge(s_rel_t, 2)
            step(nc.vector.memset(ext[:, :], 0.0))
            ready()
            step(nc.vector.tensor_copy(ext[:, first:first + 128], bank_s[0][0:AH, 0:128]))
            step(nc.vector.tensor_copy(ext[:, first + 128:first + 128 + r1], bank_s[1][0:AH, 0:r1]))
            ready()
            step(nc.vector.tensor_scalar(ext[:, 0:first], ext[:, 0:first], ext[:, first:first + 1], None, ALU.add))
            e = first + 2 * MAX_DIST - 1
            step(nc.vector.tensor_scalar(ext[:, e:], ext[:, e:], ext[:, e - 1:e], None, ALU.add))
            ready()
            nc.vector.tensor_copy(ext[:, e:e + 1], ext[:, e + 1:e + 2]).then_inc(s_ext, 1)
            dve.wait_ge(s_stage1, 9 * 16)
            for st in (stage_a, stage_c):
                nc.vector.tensor_scalar(st[:, 0:AH * AD], st[:, 0:AH * AD], float(AD) ** -0.5, None,
                                        ALU.mult).then_inc(s_staged, 1)

            def split_weights(tiles, first, n):
                for i, st in enumerate((stage_a, stage_c)):
                    dve.wait_ge(s_whi, first + i + 1)
                    for half in range(2):
                        cols = slice(half * (n // 2), (half + 1) * (n // 2))
                        nc.vector.tensor_tensor(tiles[2 * i + 1][:, cols], st[:, cols],
                                                tiles[2 * i][:, cols].bitcast(F32), ALU.subtract).then_inc(s_wlo, 1)

            dve.wait_ge(s_staged, 2)
            split_weights(w1, 0, W1_W)

            dve.wait_ge(s_stage2, 12 * 16)
            for i, (st, rows) in enumerate(((stage_a, 128), (stage_c, 128), (bqk, ROWS))):
                view = st[0:rows, 0:QK_W].rearrange("p (h d) -> p h d", d=FD)
                step(nc.vector.reduce_sum(setup_mean[0:rows, :], view, AX.X))
                ready()
                step(nc.vector.tensor_scalar(setup_mean[0:rows, :], setup_mean[0:rows, :], 1.0 / FD, None, ALU.mult))
                ready()
                ins = nc.vector.tensor_tensor(view, view, setup_mean[0:rows, :].unsqueeze(2)
                                              .to_broadcast([rows, 2 * FH, FD]), ALU.subtract)
                if i < 2:
                    ins.then_inc(s_staged, 1)
                    dve.wait_ge(s_staged, 3 + i)
                else:
                    step(ins)
            split_weights(w2, 2, W2_W)
            step(nc.vector.memset(gexp[:, :, 4 + ROUTED:], -1.0))
            step(nc.vector.memset(gtop[:, :, :], -1.0))
            ready()
            dve.wait_ge(s_dist, 9 * 16)

            def statistics(h, n):
                for r in range(TILES):
                    step(nc.vector.bn_stats(bn[n][:, r, :], h[:, r, :]))
                ready(apart=True)
                for r in range(TILES):
                    step(nc.vector.bn_aggr(mv[n][:, r, :], bn[n][:, r, :]))
                ready()
                nc.vector.tensor_scalar(var[n][:, :], mv[n][:, :, 1], LN_EPS, None, ALU.add).then_inc(s_var[n], 1)

            def normalise(h, n, img):
                dve.wait_ge(s_rstd[n], img + 1)
                for r in range(TILES):
                    step(nc.vector.tensor_scalar(xn[:, r, 0:DIM], h[:, r, :], mv[n][:, r, 0:1],
                                                 rstd[n][:, r:r + 1], ALU.subtract, ALU.mult))
                ready()
                nc.vector.tensor_copy(xn[:, :, DIM:], xn[:, :, 128:DIM]).then_inc(s_xn[n], 1)

            def split_lo(t, name, n, img):
                dve.wait_ge(s_xhi[n], img + 1)
                bank = q_bank(name)
                step(nc.vector.tensor_tensor(xl[n][:, :], bank[:, 0:COLS], xh[n][:, 0, :].bitcast(F32), ALU.subtract))
                nc.vector.tensor_tensor(xh[n][64:128, 1, :], bank[64:128, COLS:2 * COLS],
                                        xh[n][64:128, 1, :].bitcast(F32), ALU.subtract).then_inc(s_xlo[n], 1)
                q_free(dve, name, s_xlo[n], img + 1)

            two = lambda a: a[:, :, 0:4].rearrange("p t (s n) -> p t s n", s=2)
            b2 = lambda a: a[:, :, 0:2].unsqueeze(3).to_broadcast([ROWS, TILES, 2, 2])
            b10 = lambda a: a.to_broadcast([ROWS, TILES, ROUTED])

            def add_bias(t, name):
                kind, r, c = name
                q_full(dve, t, name)
                if kind == "qk2":
                    img = t.k if name in EARLY else t.k - 1
                    cols, done, n = slice(c * CHUNK, (c + 1) * CHUNK), s_qk2, ev(img, 6, r * 3 + c)
                    nc.vector.tensor_tensor(qk2[:, r, cols], q_bank(name)[0:ROWS, :], bqk[:, cols],
                                            ALU.add).then_inc(s_qk2, 1)
                else:
                    cols, done, n = slice(c * VCHUNK, (c + 1) * VCHUNK), s_v2, ev(t.k - 1, 4, V2_ORDER.index((r, c)))
                    if (r, c) == V2_ORDER[0]:
                        dve.wait_ge(s_pv, head_ev(t, -1))
                    nc.vector.tensor_tensor(v2[:, r, cols], q_bank(name)[0:ROWS, 0:VCHUNK], bv[:, cols],
                                            ALU.add).then_inc(s_v2, 1)
                    if c == 1:
                        step(nc.vector.tensor_copy(glog[:, r, 0:GATES_W], q_bank(name)[0:ROWS, VCHUNK:VCHUNK + GATES_W]))
                        ready()
                q_free(dve, name, done, n)

            def v_copy(t, r):
                name = ("v1", r, 0)
                q_full(dve, t, name)
                dve.wait_ge(s_pv, head_ev(t, AH - 1))
                nc.vector.tensor_copy(v1[:, r, 0:VCHUNK], q_bank(name)[0:ROWS, 0:VCHUNK]).then_inc(s_v1[0], 1)
                q_free(dve, name, s_v1[0], ev(t.k + 1, TILES, r))

            def high_parts(t, f):
                j, a = f // 2, f % 2
                own, other = rows_of_pair(a)
                dve.wait_ge(s_ft, ev(t.k - 1, FH, 2 * j + 1))
                dve.wait_ge(s_score, head_ev(t, AH + 2 * (j - 2) + 1 if j >= 2 else 2 * (j - 2) + 1))
                nc.vector.tensor_copy(stack[j % 2][a][other, 1, :], turned_qk[j % 2][own, 1, :])
                nc.vector.tensor_copy(stack[j % 2][a][own, 0:2, :], turned_qk[j % 2][own, :, :]).then_inc(s_high, 1)

            def variance(t, n):
                r, half = n // 2, slice(n % 2 * FH, (n % 2 + 1) * FH)
                dve.wait_ge(s_sq, ev(t.k - 1, 4, n))
                nc.vector.reduce_sum(ss[:, r, half], sq[:, :].rearrange("p (h d) -> p h d", d=FD),
                                     AX.X).then_inc(s_ss, 1)
                dve.wait_ge(s_ss, ev(t.k - 1, 4, n))
                nc.vector.tensor_scalar(ss[:, r, half], ss[:, r, half], 1.0 / FD, LN_EPS, ALU.mult,
                                        ALU.add).then_inc(s_qvar, 1)

            def normalise_qk(t, r):
                dve.wait_ge(s_qrstd, ev(t.k - 1, 4, 2 * r + 1))
                view = qk2[:, r, :].rearrange("p (h d) -> p h d", d=FD)
                nc.vector.tensor_tensor(view, view, ss[:, r, :].unsqueeze(2).to_broadcast([ROWS, 2 * FH, FD]),
                                        ALU.mult).then_inc(s_qn, 1)

            def gate_logits(t):
                lg = glog
                step(nc.vector.tensor_reduce(gmax[:, :, 0:2], two(lg), AX.X, ALU.max))
                step(nc.vector.tensor_reduce(gmax[:, :, 2:3], lg[:, :, 4:14], AX.X, ALU.max))
                ready()
                step(nc.vector.tensor_tensor(two(lg), two(lg), b2(gmax), ALU.subtract))
                ready()
                nc.vector.tensor_tensor(lg[:, :, 4:14], lg[:, :, 4:14], b10(gmax[:, :, 2:3]),
                                        ALU.subtract).then_inc(s_glog, 1)

            def gates_select(t):
                dve.wait_ge(s_gexp, t.k)
                ge = gexp
                step(nc.vector.tensor_reduce(gsum[:, :, 0:2], two(ge), AX.X, ALU.add))
                step(nc.vector.tensor_reduce(gsum[:, :, 2:3], ge[:, :, 4:14], AX.X, ALU.add))
                ready()
                step(nc.vector.reciprocal(gsum[:, :, :], gsum[:, :, :]))
                ready()
                step(nc.vector.tensor_tensor(two(glog), two(ge), b2(gsum), ALU.mult))
                step(nc.vector.tensor_tensor(ge[:, :, 4:14], ge[:, :, 4:14], b10(gsum[:, :, 2:3]), ALU.mult))
                ready(apart=True)
                for r in range(TILES):
                    step(nc.vector.max(gtop[:, r, :], ge[:, r, 4:14]))
                ready()
                step(nc.vector.memset(gtop[:, :, TOPK:], -1.0))
                ready(apart=True)
                for r in range(TILES):
                    step(nc.vector.match_replace(gcut[:, r, :], gtop[:, r, :], ge[:, r, 4:20], -2.0))
                ready()
                step(nc.vector.scalar_tensor_tensor(out=gsel[:, :, :], in0=gcut[:, :, 0:ROUTED], scalar=-1.5,
                                                    in1=ge[:, :, 4:14], op0=ALU.is_lt, op1=ALU.mult))

            def gates_scale(t):
                ready()
                step(nc.vector.tensor_reduce(gden[:, :], gsel[:, :, :], AX.X, ALU.add))
                ready()
                step(nc.vector.tensor_scalar(gden[:, :], gden[:, :], FLT_EPS, None, ALU.max))
                ready()
                step(nc.vector.reciprocal(gden[:, :], gden[:, :]))
                ready()
                step(nc.vector.scalar_tensor_tensor(out=gden[:, :], in0=gden[:, :], scalar=2.0 * TOPK,
                                                    in1=glog[:, :, 1], op0=ALU.mult, op1=ALU.mult))
                step(nc.vector.scalar_tensor_tensor(out=gate[:, :, 0:SHARED], in0=glog[:, :, 2:4],
                                                    scalar=2.0 * SHARED,
                                                    in1=glog[:, :, 0:1].to_broadcast([ROWS, TILES, SHARED]),
                                                    op0=ALU.mult, op1=ALU.mult))
                ready()
                step(nc.vector.tensor_tensor(gate[:, :, SHARED:], gsel[:, :, :],
                                             gden[:, :].unsqueeze(2).to_broadcast([ROWS, TILES, ROUTED]),
                                             ALU.mult))
                ready()

            def maxes(t, g):
                if not t.head(g):
                    return pass_over(dve, s_max, head_ev(t, g))
                dve.wait_ge(s_score, head_ev(t, g))
                bank = bank_s[g % 2]
                nm = negmax[g % 4]
                if g < AH:
                    dve.wait_ge(s_pt, head_ev(t, g - 4))
                    dve.sem_inc(s_apart, 1)
                    for r in range(TILES):
                        ins = nc.vector.tensor_tensor_reduce(
                            prob[g % 4][:, r, 0:SEQ], bank[0:ROWS, r * COLS:r * COLS + SEQ],
                            dist[:, r, g, 0:SEQ], 1.0, -3.0e38, ALU.add, ALU.max, nm[:, 2 + r:3 + r])
                    ins.then_inc(s_logit, 1)
                    dve.wait_ge(s_logit, ev(t.k, AH, g))
                    nc.vector.tensor_scalar(nm[:, 0:TILES], nm[:, 2:4], -1.0, None, ALU.mult).then_inc(s_max, 1)
                else:
                    dve.wait_ge(s_exp, head_ev(t, g - 4))
                    nc.vector.tensor_reduce(nm[:, 0:TILES], bank[0:ROWS, 0:2 * COLS]
                                            .rearrange("p (t k) -> p t k", t=TILES)[:, :, 0:SEQ],
                                            AX.X, ALU.max, negate=True).then_inc(s_max, 1)

            def recip(t, g):
                if t.head(g) is None:
                    return None
                if not t.head(g):
                    return pass_over(dve, s_rec, head_ev(t, g))
                dve.wait_ge(s_exp, head_ev(t, g))
                dve.wait_ge(s_prob, head_ev(t, g - 4))
                if g % HEADS < AH:
                    nc.vector.reciprocal(rec[g % 4][:, :], psumr[g % 4][:, :]).then_inc(s_rec, 1)
                else:
                    step(nc.vector.reciprocal(psumr[g % 4][:, :], psumr[g % 4][:, :]))
                    ready()
                    nc.vector.tensor_tensor(rec[g % 4][:, :], psumr[g % 4][:, :], gate[:, :, g % HEADS - AH],
                                            ALU.mult).then_inc(s_rec, 1)

            def new_h(t, r):
                q_full(dve, t, ("tok", r))
                step(nc.vector.tensor_tensor(h0[1 - t.p][0:HALF, r, :], q_bank(("tok", r))[0:HALF, 0:DIM],
                                             posb[0:HALF, r, :], ALU.add))
                q_free(dve, ("tok", r), s_dve, chain.value())
                if r == 1:
                    statistics(h0[1 - t.p], 0)

            def attended(t, r):
                q_full(dve, t, ("out", r))
                if r == 0 and not (isinstance(t.k, int) and t.k == 0):
                    dve.wait_ge(s_h1b, t.k)
                nc.vector.tensor_tensor(h1[:, r, :], q_bank(("out", r))[0:ROWS, 0:DIM], h0[t.p][:, r, :],
                                        ALU.add).then_inc(s_h1, 1)
                q_free(dve, ("out", r), s_h1, ev(t.k, TILES, r))
                if r == 1:
                    statistics(h1, 1)

            def output(t, r):
                q_full(dve, t, ("proj", r))
                if r == 0:
                    dve.wait_ge(s_h1b, t.k - 1)
                nc.vector.tensor_tensor(h1b[t.p][:, r, :], q_bank(("proj", r))[0:ROWS, 0:DIM], h1b[t.p][:, r, :],
                                        ALU.add).then_inc(s_osb, 1)
                q_free(dve, ("proj", r), s_osb, ev(t.k - 2, TILES, r) + 1)

            def turn(t):
                for s in steps_of(t):
                    for name in FILL.get(s, []):
                        if name[0] in ("qk2", "v2") and t.has(name):
                            add_bias(t, name)
                        if name[0] == "proj" and t.proj:
                            output(t, name[1])
                        if name[0] == "tok" and t.tok:
                            new_h(t, name[1])
                        if name[0] == "out" and t.att:
                            attended(t, name[1])
                        if name[0] == "v1" and name[2] == 0 and t.tok:
                            v_copy(t, name[1])
                    if s == 10 and t.tok:
                        normalise(h0[1 - t.p], 0, t.k + 1)
                    if s == 16 and t.att:
                        normalise(h1, 1, t.k)
                    for name in PREP.get(s, []):
                        if name[0] == "x1t" and t.tok:
                            split_lo(t, name, 0, t.k + 1)
                        if name[0] == "x2t" and t.att:
                            split_lo(t, name, 1, t.k)
                    if s < AH:
                        recip(t, s - 1)
                    maxes(t, s)
                    if s >= AH:
                        recip(t, s - 1)
                    if t.ffn:
                        for f in STACK_STEPS.get(s, []):
                            high_parts(t, f)
                        if 1 <= s <= 4:
                            variance(t, s - 1)
                        if s in (5, 6):
                            normalise_qk(t, s - 5)
                        if s == 5:
                            gate_logits(t)
                        if s == 7:
                            gates_select(t)
                        if s == 8:
                            gates_scale(t)

            for s in (s_max, s_rec, s_osb):
                dve.sem_inc(s, 1)
            for t in turns_before():
                turn(t)
            base = chain.n
            with dve.Fori(0, LOOPS) as it:
                for p in range(2):
                    chain.base, chain.n = base + (it * 2 + p) * DVE_STEPS, 0
                    turn(loop_turn(it, p))
                    assert chain.n == DVE_STEPS, chain.n
            chain.base, chain.n = base + 2 * LOOPS * DVE_STEPS, 0
            for t in turns_after():
                turn(t)

        @block.gpsimd
        def _(pool):
            nc.gpsimd.memset(ident[:, :], 0.0).then_inc(s_ident, 1)
            nc.gpsimd.memset(eps_pow[:, :], -0.5).then_inc(s_ident, 1)
            pool.wait_ge(s_ident, 2)
            nc.gpsimd.affine_select(out=ident[:, :], in_=ident[:, :], compare_op=ALU.not_equal, fill=1.0,
                                    base=0, pattern=[[-1, 128]], channel_multiplier=1).then_inc(s_ident, 1)
            zeros = [posb[96:ROWS, 1, :], h0[0][96:ROWS, 1, :], dist[:, 1, :, :]]
            zeros += [stack[i][a][64 * (1 - a):64 * (2 - a), 2, :].bitcast(F32) for i in range(2) for a in range(2)]
            zeros += [pr[:, :, SEQ:COLS] for pr in prob]
            for n, z in enumerate(zeros):
                pool.wait_ge(s_ident, 3 + n)
                nc.gpsimd.memset(z, 0.0).then_inc(s_ident, 1)
            pool.wait_ge(s_ident, N_ZEROED)

            def rsqrt(ready, value, done, a, b, n):
                pool.wait_ge(ready, value)
                nc.gpsimd.tensor_tensor(b, a, eps_pow[0:ROWS, 0:n], ALU.pow).then_inc(done, 1)

            def scale(t, g):
                if t.head(g) is None:
                    return None
                if not t.head(g):
                    return pass_over(pool, s_prob, head_ev(t, g))
                pool.wait_ge(s_rec, head_ev(t, g))
                pr = prob[g % 4][:, :, 0:SEQ]
                nc.gpsimd.tensor_tensor(pr, pr, rec[g % 4][:, :].unsqueeze(2).to_broadcast([ROWS, TILES, SEQ]),
                                        ALU.mult).then_inc(s_prob, 1)

            def low_parts(t, f, s):
                j, a = f // 2, f % 2
                own, other = rows_of_pair(a)
                st = stack[j % 2][a]
                pool.wait_ge(s_high, ev(t.k - 1, FH, f))
                pool.wait_ge(s_prob, head_ev(t, s - 1))
                nc.gpsimd.tensor_tensor(st[other, 0, :], turned_qk[j % 2][own, 0, :], st[own, 0, :].bitcast(F32),
                                        ALU.subtract).then_inc(s_lowq, 1)
                pool.wait_ge(s_lowq, ev(t.k - 1, FH, f))
                nc.gpsimd.tensor_tensor(st[own, 2, :], turned_qk[j % 2][own, 1, :], st[own, 1, :].bitcast(F32),
                                        ALU.subtract).then_inc(s_low, 1)
                pool.wait_ge(s_low, ev(t.k - 1, FH, f))

            def turn(t):
                for s in steps_of(t):
                    if s == 8 and t.tok:
                        rsqrt(s_var[0], t.k + 2, s_rstd[0], var[0][:, :], rstd[0][:, :], TILES)
                    if s == 14 and t.att:
                        rsqrt(s_var[1], t.k + 1, s_rstd[1], var[1][:, :], rstd[1][:, :], TILES)
                    scale(t, s - 1)
                    if 1 <= s <= 4 and t.ffn:
                        r, half = (s - 1) // 2, slice((s - 1) % 2 * FH, ((s - 1) % 2 + 1) * FH)
                        rsqrt(s_qvar, ev(t.k - 1, 4, s - 1), s_qrstd, ss[:, r, half], ss[:, r, half], FH)
                    if t.ffn:
                        for f in STACK_STEPS.get(s, []):
                            low_parts(t, f, s)
                    if s == 18 and t.att:
                        pool.wait_ge(s_h1, ev(t.k, TILES, 1))
                        if t.proj:
                            pool.wait_ge(s_out[t.p], (t.half - 1) * 48 + 64)
                        nc.gpsimd.tensor_tensor(h1b[t.p][:, :, :], h1[:, :, :],
                                                bproj[:, :].unsqueeze(1).to_broadcast([ROWS, TILES, DIM]),
                                                ALU.add).then_inc(s_h1b, 1)

            pool.sem_inc(s_prob, 1)
            for t in turns_before():
                turn(t)
            with pool.Fori(0, LOOPS) as it:
                for p in range(2):
                    turn(loop_turn(it, p))
            for t in turns_after():
                turn(t)


_INS = ["x", "L0_tok_W", "L0_tok_b", "L0_tok_class_token", "L0_tok_pos_embed", "L0_attn_w_q", "L0_attn_w_k",
        "L0_attn_w_v", "L0_attn_w_o", "L0_attn_rel_emb", "L0_ffn_qkv_w", "L0_ffn_qkv_b", "L0_ffn_q_norm_w",
        "L0_ffn_q_norm_b", "L0_ffn_k_norm_w", "L0_ffn_k_norm_b", "L0_ffn_wg_w", "L0_ffn_wg0_w", "L0_ffn_wg1_w",
        "L0_ffn_proj_w", "L0_ffn_proj_b"]
_OUTS = [((IMAGES, SEQ, DIM), "float32")]


def kernel(**inputs):
    import numpy as _np
    import concourse.bacc as _bacc
    from concourse import mybir as _mybir
    from concourse.bass_utils import run_bass_kernel_spmd as _run

    nc = _bacc.Bacc("TRN2", target_bir_lowering=False, num_devices=1)
    arrays, args = {}, []
    for name in _INS:
        a = _np.ascontiguousarray(inputs[name])
        arrays[f"in_{name}_dram"] = a
        args.append(nc.dram_tensor(f"in_{name}_dram", a.shape, _mybir.dt.from_np(a.dtype), kind="ExternalInput").ap())
    for i, (shape, dtype) in enumerate(_OUTS):
        dt = _mybir.dt.from_np(_np.dtype(dtype))
        args.append(nc.dram_tensor(f"out_{i}_dram", shape, dt, kind="ExternalOutput").ap())
    vit_kernel(nc, *args)
    r = _run(nc, [arrays], core_ids=[0])
    got = tuple(r.results[0][f"out_{i}_dram"] for i in range(len(_OUTS)))
    return got[0]
```
